# Optimizing a Trainium2 kernel written in Bass

```python
import numpy as np
import jax
import jax.numpy as jnp

def _softmax(x, axis=-1):
    return jax.nn.softmax(x, axis=axis)

def _gelu(x):
    return jax.nn.gelu(x, approximate=True)

def _silu(x):
    return jax.nn.silu(x)

def _sigmoid(x):
    return jax.nn.sigmoid(x)

def _layernorm(x, axis=-1, eps=1e-05):
    m = jnp.mean(x, axis=axis, keepdims=True)
    v = jnp.var(x, axis=axis, keepdims=True)
    return (x - m) / jnp.sqrt(v + eps)

def _scatter_add(tgt, idx, src, axis=0):
    return tgt.at[idx].add(src)

def _segment_sum(src, seg, n):
    return jax.ops.segment_sum(src, seg, n)
kernel_name = 'mk_prb_d1_jaxref_r2_11a9bf'

def setup_inputs(seed: int=0):
    np.random.seed(seed)
    _w = jnp.asarray

    def _L0_attn_setup():
        import jax, jax.numpy as jnp
        import numpy as np
        B, S, E = (2, 1024, 512)
        H, W_SIZE = (16, 128)
        D = E // H
        key = jax.random.key(seed)
        ks = jax.random.split(key, 7)
        std = 1.0 / np.sqrt(E)
        return {'x': jax.random.normal(ks[0], (B, S, E), dtype=jnp.float32), 'Wq': jax.random.normal(ks[1], (E, E), dtype=jnp.float32) * std, 'bq': jax.random.normal(ks[2], (E,), dtype=jnp.float32) * std, 'Wk': jax.random.normal(ks[3], (E, E), dtype=jnp.float32) * std, 'bk': jax.random.normal(ks[4], (E,), dtype=jnp.float32) * std, 'Wv': jax.random.normal(ks[5], (E, E), dtype=jnp.float32) * std, 'bv': jax.random.normal(ks[6], (E,), dtype=jnp.float32) * std}
    _L0_attn_in = _L0_attn_setup()

    def _L0_ffn_setup():
        import math
        import jax, jax.numpy as jnp
        import numpy as np
        CAPACITY_FACTOR = 1.25
        key = jax.random.key(seed)
        ks = jax.random.split(key, 5)
        B, S, H, F, E = (4, 2048, 512, 512, 32)
        scale_in = 1.0 / math.sqrt(H)
        scale_mid = 1.0 / math.sqrt(F)
        return {'x': jax.random.normal(ks[0], (B, S, H), dtype=jnp.float32), 'w_router': jax.random.normal(ks[1], (H, E), dtype=jnp.float32) * scale_in, 'w_gate': jax.random.normal(ks[2], (E, H, F), dtype=jnp.float32) * scale_in, 'w_up': jax.random.normal(ks[3], (E, H, F), dtype=jnp.float32) * scale_in, 'w_down': jax.random.normal(ks[4], (E, F, H), dtype=jnp.float32) * scale_mid}
    _L0_ffn_in = _L0_ffn_setup()
    _d = {'L0_attn_x': _L0_attn_in['x'], 'L0_attn_Wq': _L0_attn_in['Wq'], 'L0_attn_bq': _L0_attn_in['bq'], 'L0_attn_Wk': _L0_attn_in['Wk'], 'L0_attn_bk': _L0_attn_in['bk'], 'L0_attn_Wv': _L0_attn_in['Wv'], 'L0_attn_bv': _L0_attn_in['bv'], 'L0_ffn_w_router': _L0_ffn_in['w_router'], 'L0_ffn_w_gate': _L0_ffn_in['w_gate'], 'L0_ffn_w_up': _L0_ffn_in['w_up'], 'L0_ffn_w_down': _L0_ffn_in['w_down']}
    _x0 = _d['L0_attn_x']
    _d['L0_attn_x'] = jax.random.normal(jax.random.fold_in(jax.random.key(seed), 1), (8, 1024, 512), dtype=_x0.dtype)
    del _x0
    return _d

def reference(L0_attn_x, L0_attn_Wq, L0_attn_bq, L0_attn_Wk, L0_attn_bk, L0_attn_Wv, L0_attn_bv, L0_ffn_w_router, L0_ffn_w_gate, L0_ffn_w_up, L0_ffn_w_down):

    def _L0_attn_ref(x, Wq, bq, Wk, bk, Wv, bv):
        import jax, jax.numpy as jnp
        import numpy as np
        B, S, E = (2, 1024, 512)
        H, W_SIZE = (16, 128)
        D = E // H
        b, s, e = x.shape
        scale = jnp.float32(D) ** (-0.5)
        q = (x @ Wq.T + bq).reshape(b, H, s, D)
        k = (x @ Wk.T + bk).reshape(b, H, s, D)
        v = (x @ Wv.T + bv).reshape(b, H, s, D)
        i = jnp.arange(s)[:, None]
        j = jnp.arange(s)[None, :]
        mask = (j >= i - W_SIZE) & (j < i + W_SIZE)
        qk = jnp.einsum('bhid,bhjd->bhij', q, k)
        scores = jnp.where(mask, qk, 0.0) * scale
        probs = jax.nn.softmax(scores, axis=-1)
        out = jnp.einsum('bhij,bhjd->bhid', probs, v)
        out = out.transpose(0, 2, 1, 3).reshape(b, s, e)
        return out

    def _L0_ffn_ref(x, w_router, w_gate, w_up, w_down):
        import math
        import jax, jax.numpy as jnp
        import numpy as np
        CAPACITY_FACTOR = 1.25
        B, S, H = x.shape
        E = w_gate.shape[0]
        T = B * S
        C = int(math.ceil(CAPACITY_FACTOR * T / E))
        xt = x.reshape(T, H)
        logits = xt @ w_router
        probs = jax.nn.softmax(logits, axis=-1)
        top1 = jnp.argmax(probs, axis=-1)
        gate = jnp.take_along_axis(probs, top1[:, None], axis=1)[:, 0]
        onehot = jax.nn.one_hot(top1, E, dtype=jnp.int32)
        pos = jnp.cumsum(onehot, axis=0)[jnp.arange(T), top1] - 1
        accepted = pos < C
        slot = jnp.where(accepted, top1 * C + pos, E * C)
        buf = jnp.zeros((E * C + 1, H), dtype=x.dtype).at[slot].set(xt)
        buf = buf[:E * C].reshape(E, C, H)
        g = jnp.einsum('ech,ehf->ecf', buf, w_gate)
        u = jnp.einsum('ech,ehf->ecf', buf, w_up)
        y = jnp.einsum('ecf,efh->ech', jax.nn.silu(g) * u, w_down)
        out_tok = y.reshape(E * C, H)[jnp.clip(slot, 0, E * C - 1)]
        out_tok = jnp.where(accepted[:, None], out_tok * gate[:, None], 0.0)
        return (xt + out_tok).reshape(B, S, H)
    x = L0_attn_x
    xn = _layernorm(x, axis=-1)
    x = x + _L0_attn_ref(xn, L0_attn_Wq, L0_attn_bq, L0_attn_Wk, L0_attn_bk, L0_attn_Wv, L0_attn_bv) + _L0_ffn_ref(xn, L0_ffn_w_router, L0_ffn_w_gate, L0_ffn_w_up, L0_ffn_w_down)
    return x

_drawn_inputs = setup_inputs


def setup_inputs(seed=0):
    import zlib

    import numpy as np

    out = dict(_drawn_inputs(seed))
    spreads = {}
    factors = {'L0_attn_Wq': 2.833, 'L0_attn_bq': 8.0, 'L0_attn_bk': 8.0, 'L0_attn_bv': 8.0}
    for name, (base, spread) in spreads.items():
        noise = np.random.default_rng([zlib.crc32(name.encode()), seed]).standard_normal(out[name].shape)
        drawn = base * np.exp(spread * noise) if base else spread * noise
        out[name] = jnp.asarray(drawn.astype(out[name].dtype))
    for name, factor in factors.items():
        out[name] = (out[name] * factor).astype(out[name].dtype)
    return out
```

```python
from contextlib import ExitStack

import numpy as np
import concourse.bass as bass
from concourse import mybir

ALU = mybir.AluOpType
ACT = mybir.ActivationFunctionType
F32 = mybir.dt.float32
F32R = mybir.dt.float32r
BF16 = mybir.dt.bfloat16
U32 = mybir.dt.uint32
I32 = mybir.dt.int32
AX = mybir.AxisListType

P = 128


class Counter:

    def __init__(self, handle):
        self.handle = handle
        self.value = 0


class Queue:

    def __init__(self):
        self.steps = []
        self.waited = {}

    def wait(self, *marks):
        for counter, value in marks:
            if self.waited.get(counter, 0) < value:
                self.waited[counter] = value
                self.steps.append((counter.handle, value))

    def do(self, emit, counter=None, by=1):
        if counter is None:
            self.steps.append((emit,))
            return None
        counter.value += by
        self.steps.append((emit, counter.handle, by))
        return (counter, counter.value)

    def play(self, engine):
        for step in self.steps:
            if len(step) == 2:
                engine.wait_ge(step[0], step[1])
            elif len(step) == 1:
                step[0](engine)
            else:
                step[0](engine).then_inc(step[1], step[2])


def build(nc, x, Wq, bq, Wk, bk, Wv, bv, w_router, w_gate, w_up, w_down, out):
    B, S, E = x.shape
    H = 16
    D = E // H
    CH = E // D
    HT = S // CH
    BAND = 128
    TOK = B * S
    NX, _, FF = w_gate.shape
    CAP = -(-5 * TOK // (4 * NX))
    SLOTS = NX * CAP
    KT = E // P
    QH = 4
    QT = QH * HT
    NQ = TOK // QT
    QB = H // QH
    NT = S // P
    TT = P // CH
    TPQ = QT // P
    XR = 2
    PR = 4
    SR = 8
    SCALE = float(D) ** -0.5
    FAR = float(1 << 20)
    assert BAND == P and QT == 256 and TT == 8 and FF == E and E == 512

    Q = {n: Queue() for n in ("pe", "act", "dve", "pool", "sp")}
    pe, act, dve, pool, sp = (Q[n] for n in ("pe", "act", "dve", "pool", "sp"))

    x_rows = x.rearrange("b s e -> (b s) e")
    out_rows = out.rearrange("b s e -> (b s) e")
    xn_rows = nc.dram_tensor("xn_rows", [TOK, E], F32, kind="Internal").ap()
    sum_rows = nc.dram_tensor("sum_rows", [TOK, E], F32, kind="Internal").ap()
    base_rows = nc.dram_tensor("base_rows", [TOK, E], F32, kind="Internal").ap()
    slot_table = nc.dram_tensor("slot_table", [SLOTS, 2], F32, kind="Internal").ap()

    with ExitStack() as ctx:
        def sem(name):
            return Counter(ctx.enter_context(nc.semaphore(name)))

        def sb(name, shape, dt=F32, c=None):
            return (c or ctx).enter_context(nc.sbuf_tensor(name, shape, dt))

        def ps(name, shape):
            return ctx.enter_context(nc.psum_tensor(name, shape, F32))

        p_score = ps("p_score", [P, 2, 512])
        p_turn = ps("p_turn", [P, 2, 512])
        p_att = ps("p_att", [P, 512])
        p_proj = ps("p_proj", [P, 2, 512])
        p_misc = ps("p_misc", [P, 512])

        ident = sb("ident", [P, P])
        slot_of = sb("slot_of", [P, TOK // P], U32)
        id_gate = sb("id_gate", [P, TOK // P, 2])

        s_const = sem("s_const")
        s_scatter = sem("s_scatter")
        s_store = [sem(f"s_store{i}") for i in range(NT)]
        s_base = [sem(f"s_base{i}") for i in range(NT)]
        s_sum = [sem(f"s_sum{i}") for i in range(XR)]
        s_xnst = [sem(f"s_xnst{i}") for i in range(TPQ)]

        c1 = ctx.enter_context(ExitStack())

        def sb1(name, shape, dt=F32):
            return sb(name, shape, dt, c1)

        wt = sb1("wt", [P, 3, 2, KT, E], F32R)
        bias = sb1("bias", [P, 3, KT])
        wr = sb1("wr", [P, KT, NX])
        wr_parts = sb1("wr_parts", [P, 2, KT, NX], F32R)
        mask = sb1("mask", [P, CH, 3 * TT])
        q_land = sb1("q_land", [96, CH, QT], F32R)
        qn = sb1("qn", [96, QT, CH], F32R)
        v_land = sb1("v_land", [P, CH, HT])
        v_nat = sb1("v_nat", [P, HT, CH])
        ks = [sb1(f"ks{i}", [96, CH, QT], F32R) for i in range(2)]
        stage = sb1("stage", [P, 2, KT, QT], F32R)
        stage_v = sb1("stage_v", [P, KT, QT])
        xt = sb1("xt", [P, 2, KT, QT], F32R)
        xn = sb1("xn", [P, TPQ, E])
        res = sb1("res", [P, XR, E])
        late = sb1("late", [P, E])
        ao = sb1("ao", [P, NT, E])
        prob = sb1("prob", [P, SR, 3 * P])
        probT = sb1("probT", [P, PR, QH * P])
        vn = sb1("vn", [P, 2, NT, P])
        attT = sb1("attT", [P, 4 * P])
        far_e = sb1("far_e", [P, 4 * P])
        neg_max = sb1("neg_max", [P, 2, NT, QH])
        row_max = sb1("row_max", [P, 2, NT, QH])
        e_out = sb1("e_out", [P, 2, NT, QH])
        row_sum = sb1("row_sum", [P, 2, NT, QH])
        den = sb1("den", [P, 2, NT, QH])
        rden = sb1("rden", [P, 2, NT, QH])
        n_out = sb1("n_out", [P, NT, QH])
        vsum = sb1("vsum", [P, 2, NT], F32R)
        far_rows = sb1("far_rows", [2 * NT, 2, P], F32R)
        far_pick = sb1("far_pick", [2 * NT, NT])
        far_pick_r = sb1("far_pick_r", [2 * NT, NT], F32R)
        ones2 = sb1("ones2", [P, 2])
        stats = sb1("stats", [P, TPQ, 6])
        moments = sb1("moments", [P, TPQ, 2])
        rstd = sb1("rstd", [P, TPQ])
        veps = sb1("veps", [P, TPQ])
        newton = sb1("newton", [P, TPQ])
        tri = sb1("tri", [P, P], BF16)
        ones_bf = sb1("ones_bf", [P, P], BF16)
        ex_iota = sb1("ex_iota", [P, NX])
        logit = sb1("logit", [P, NX])
        top = sb1("top", [P, 8])
        top_i = sb1("top_i", [P, 8], U32)
        top_f = sb1("top_f", [P, 1])
        ntop = sb1("ntop", [P, 1])
        expl = sb1("expl", [P, NX])
        expsum = sb1("expsum", [P, 1])
        onehot = sb1("onehot", [P, 2, NX], BF16)
        seen = sb1("seen", [P, 2, NX], BF16)
        pos_junk = sb1("pos_junk", [P, NX])
        pos = sb1("pos", [P, 1])
        rej = sb1("rej", [P, 1])
        slot_f = sb1("slot_f", [P, 1])

        s_load = sem("s_load")
        s_wraw = [sem(f"s_wraw{i}") for i in range(3)]
        s_pw = sem("s_pw")
        s_aw = sem("s_aw")
        s_dw = sem("s_dw")
        s_tab = sem("s_tab")

        def fill(t, v):
            return pool.do(lambda e: e.memset(t, v), s_const)

        fill(ident[:], 0.0)
        c0 = fill(mask[:], 1.0)
        pool.wait(c0)
        pool.do(lambda e: e.affine_select(out=ident[:], in_=ident[:], compare_op=ALU.not_equal, fill=1.0, base=0,
                                          pattern=[[-1, P]], channel_multiplier=1), s_const)
        c0 = pool.do(lambda e: e.affine_select(out=mask[:], in_=mask[:], compare_op=ALU.is_ge, fill=0.0, base=0,
                                               pattern=[[1, CH], [CH, 3 * TT]], channel_multiplier=-1), s_const)
        pool.wait(c0)
        pool.do(lambda e: e.affine_select(out=mask[:], in_=mask[:], compare_op=ALU.is_gt, fill=0.0, base=2 * BAND,
                                          pattern=[[-1, CH], [-CH, 3 * TT]], channel_multiplier=1), s_const)
        fill(ones2[:], 1.0)
        fill(ones_bf[:], 1.0)
        c0 = fill(tri[:], 1.0)
        pool.wait(c0)
        pool.do(lambda e: e.affine_select(out=tri[:], in_=tri[:], compare_op=ALU.is_ge, fill=0.0, base=0,
                                          pattern=[[1, P]], channel_multiplier=-1), s_const)
        pool.do(lambda e: e.iota(ex_iota[:], pattern=[[1, NX]], base=0, channel_multiplier=0,
                                 allow_small_or_imprecise_dtypes=True), s_const)
        pool.do(lambda e: e.iota(id_gate[:, :, 0], pattern=[[P, TOK // P]], base=0, channel_multiplier=1,
                                 allow_small_or_imprecise_dtypes=True), s_const)
        c0 = fill(n_out[:], float(S - 3 * P))
        pool.wait(c0)
        fill(n_out[:, 0, :], float(S - 2 * P))
        fill(n_out[:, NT - 1, :], float(S - 2 * P))
        c0 = fill(far_pick[:], 1.0)

        def pick(base, step, fill_value):
            nonlocal c0
            pool.wait(c0)
            c0 = pool.do(lambda e: e.affine_select(out=far_pick[:], in_=far_pick[:], compare_op=ALU.not_equal,
                                                   fill=fill_value, base=base, pattern=[[step, NT]],
                                                   channel_multiplier=-1), s_const)

        for off in (-1, 0, 1, NT - 1, NT, NT + 1):
            pick(off, 1, 0.0)
        pick(NT - 1, -1000, 1.0)
        pick(NT + 1000 * (NT - 1), -1000, 1.0)
        table_init = prob[:, 0, 0:2 * SLOTS // P].rearrange("p (n two) -> p n two", two=2)
        fill(table_init[:, :, 0], FAR)
        c_const = fill(table_init[:, :, 1], 0.0)
        sp.wait(c_const)
        m_tab = sp.do(lambda e: e.dma_start(slot_table.rearrange("(p n) two -> p (n two)", p=P),
                                            prob[:, 0, 0:2 * SLOTS // P]), s_tab, 16)
        dve.wait(c_const)
        c_pick = dve.do(lambda e: e.tensor_copy(far_pick_r[:], far_pick[:]), s_dw)

        raw = [vn[:].rearrange("p a t c -> p (a t c)"), ao[:, 0:4, :].rearrange("p t e -> p (t e)"),
               ao[:, 4:8, :].rearrange("p t e -> p (t e)")]
        m_w = []
        for i, (w, b) in enumerate(((Wq, bq), (Wk, bk), (Wv, bv))):
            dst = raw[i].rearrange("p (t e) -> p t e", t=KT)
            sp.do(lambda e, dst=dst, w=w: e.dma_start(dst, w.rearrange("(t p) e -> p t e", p=P)), s_wraw[i], 16)
            m_w.append(sp.do(lambda e, i=i, b=b: e.dma_start(bias[:, i, :], b.rearrange("(t p) -> p t", p=P), allow_slow_non_contiguous=True),
                             s_wraw[i], 16))
        m_wr = sp.do(lambda e: e.dma_start(wr[:], w_router.rearrange("(k p) n -> p k n", p=P)), s_load, 16)
        dve.wait(m_wr)
        c0 = dve.do(lambda e: e.tensor_copy(wr_parts[:, 0], wr[:]), s_dw)
        dve.wait(c0)
        m_wrp = dve.do(lambda e: e.tensor_tensor(wr_parts[:, 1], wr[:], wr_parts[:, 0].bitcast(F32), ALU.subtract),
                       s_dw)

        pe.wait(c_const)
        free = [[], []]
        for i in range(3):
            pe.wait(m_w[i])
            src = raw[i].rearrange("p (t e) -> p t e", t=KT)
            for k in range(KT):
                r = (i * KT + k) % 2
                pe.wait(*free[r])
                for f in range(KT):
                    m = pe.do(lambda e, r=r, f=f, k=k, src=src: e.transpose(
                        p_turn[:, r, f * P:(f + 1) * P], src[:, f, k * P:(k + 1) * P], ident[:]),
                        s_pw if f == KT - 1 else None)
                act.wait(m)
                a = act.do(lambda e, r=r, i=i, k=k: e.activation(wt[:, i, 0, k, :], p_turn[:, r, :], ACT.Copy), s_aw)
                dve.wait(m, a)
                d = dve.do(lambda e, r=r, i=i, k=k: e.tensor_tensor(
                    wt[:, i, 1, k, :], p_turn[:, r, :], wt[:, i, 0, k, :].bitcast(F32), ALU.subtract), s_dw)
                free[r] = [a, d]
        m_weights = free[0] + free[1]

        s_x = [sem(f"s_x{i}") for i in range(XR)]
        s_q = sem("s_q")
        s_k = [sem(f"s_k{i}") for i in range(2)]
        s_v = sem("s_v")
        s_copy = sem("s_copy")
        s_ln = sem("s_ln")
        s_newton = sem("s_newton")
        s_resadd = sem("s_resadd")
        s_xturn = sem("s_xturn")
        s_xhi = sem("s_xhi")
        s_xlo = sem("s_xlo")
        s_proj = sem("s_proj")
        s_phi = sem("s_phi")
        s_plo = sem("s_plo")
        s_score = sem("s_score")
        s_masked = sem("s_masked")
        s_negm = sem("s_negm")
        s_exp = sem("s_exp")
        s_turn = sem("s_turn")
        s_turnedA = sem("s_turned_act")
        s_turnedD = sem("s_turned_dve")
        s_pv = sem("s_pv")
        s_att = sem("s_att")
        s_post = sem("s_post")
        s_pm = sem("s_pm")
        s_ma = sem("s_ma")
        s_md = sem("s_md")
        s_rt = sem("s_rt")
        s_resdone = sem("s_resdone")
        s_late = sem("s_late")

        misc_free = []
        res_free = [[] for _ in range(XR)]
        ao_free = [m_weights] * NT
        late_free = []
        m_x, m_ln, m_xadd, m_xnst, m_sum, m_rstd = {}, {}, {}, {}, {}, {}

        def load_x(tt):
            sp.wait(*res_free[tt % XR])
            m_x[tt] = sp.do(lambda e: e.dma_start(res[:, tt % XR, :], x_rows[tt * P:(tt + 1) * P, :]),
                            s_x[tt % XR], 16)

        def norm_scale(q):
            for tt in range(q * TPQ, (q + 1) * TPQ):
                j, r = tt % TPQ, tt % XR
                dve.wait(m_x[tt])
                if q:
                    dve.wait(m_rstd[q - 1])
                c = dve.do(lambda e, j=j, r=r: e.bn_stats(stats[:, j, :], res[:, r, :]), s_ln)
                dve.wait(c)
                c = dve.do(lambda e, j=j: e.bn_aggr(moments[:, j, :], stats[:, j, :]), s_ln)
            dve.wait(c)
            c = dve.do(lambda e: e.tensor_scalar(veps[:], moments[:, :, 1], 1e-5, None, ALU.add), s_ln)
            dve.wait(c)
            if q:
                dve.wait(m_ln[q * TPQ - 1])
            c = dve.do(lambda e: e.tensor_scalar(rstd[:].bitcast(I32), veps[:].bitcast(I32), -0.5,
                                                 float(0x5F3759DF), ALU.mult, ALU.add), s_ln)

            def step(emit):
                nonlocal c
                pool.wait(c)
                c = pool.do(emit, s_newton)

            for _ in range(3):
                step(lambda e: e.tensor_tensor(newton[:], rstd[:], rstd[:], ALU.mult))
                step(lambda e: e.tensor_tensor(newton[:], newton[:], veps[:], ALU.mult))
                step(lambda e: e.tensor_scalar(newton[:], newton[:], -0.5, 1.5, ALU.mult, ALU.add))
                step(lambda e: e.tensor_tensor(rstd[:], rstd[:], newton[:], ALU.mult))
            m_rstd[q] = c

        def layer_norm(tt):
            j, r = tt % TPQ, tt % XR
            dve.wait(m_rstd[tt // TPQ])
            if tt >= TPQ:
                dve.wait(m_xturn[tt - TPQ], m_xnst[tt - TPQ], m_xadd[tt - TPQ])
            m_ln[tt] = dve.do(lambda e: e.tensor_scalar(xn[:, j, :], res[:, r, :], moments[:, j, 0:1],
                                                        rstd[:, j:j + 1], ALU.subtract, ALU.mult), s_ln)
            pool.wait(m_ln[tt])
            m_xadd[tt] = pool.do(lambda e: e.tensor_tensor(res[:, r, :], res[:, r, :], xn[:, j, :], ALU.add),
                                 s_resadd)
            sp.wait(m_ln[tt])
            sp.wait(m_xadd[tt])
            m_sum[tt] = sp.do(lambda e: e.dma_start(sum_rows[tt * P:(tt + 1) * P, :], res[:, r, :]), s_sum[r], 16)
            res_free[r] = [m_sum[tt]]
            m_xnst[tt] = sp.do(lambda e: e.dma_start(xn_rows[tt * P:(tt + 1) * P, :], xn[:, j, :]), s_xnst[j], 16)

        m_xturn, m_xparts = {}, {}

        def turn_x(tt):
            nonlocal misc_free
            j = tt % TPQ
            pe.wait(m_ln[tt], *misc_free)
            for k in range(KT):
                m = pe.do(lambda e, k=k: e.transpose(p_misc[:, k * P:(k + 1) * P], xn[:, j, k * P:(k + 1) * P],
                                                     ident[:]), s_pm if k == KT - 1 else None)
            m_xturn[tt] = m
            src = p_misc[:].rearrange("p (k t) -> p k t", k=KT)
            act.wait(m)
            if tt >= TPQ:
                act.wait(last_proj[tt // TPQ - 1])
            a = act.do(lambda e: e.activation(xt[:, 0, :, j * P:(j + 1) * P], src, ACT.Copy), s_ma)
            dve.wait(a)
            d = dve.do(lambda e: e.tensor_tensor(xt[:, 1, :, j * P:(j + 1) * P], src,
                                                 xt[:, 0, :, j * P:(j + 1) * P].bitcast(F32), ALU.subtract), s_md)
            misc_free = [a, d]
            m_xparts[tt] = [a, d]

        last_proj = {}
        rt = {}

        def route(tt):
            nonlocal misc_free
            j = tt % TPQ
            pe.wait(m_wrp, *m_xparts[tt], *misc_free)
            terms = [(k, a, b) for k in range(KT) for a in (0, 1) for b in (0, 1)]
            for n, (k, a, b) in enumerate(terms):
                m = pe.do(lambda e, n=n, k=k, a=a, b=b: e.matmul(
                    p_misc[:, 0:NX], xt[:, a, k, j * P:(j + 1) * P], wr_parts[:, b, k, :],
                    start=n == 0, stop=n == len(terms) - 1), s_pm if n == len(terms) - 1 else None)

            def step(emit, *marks, counter=s_rt):
                dve.wait(*marks)
                return dve.do(emit, counter)

            c = step(lambda e: e.tensor_copy(logit[:], p_misc[:, 0:NX]), m, *rt.get("exp", []))
            misc_free = [c]
            c = step(lambda e: e.max(top[:], logit[:]), c)
            step(lambda e: e.tensor_scalar(ntop[:], top[:, 0:1], -1.0, None, ALU.mult), c)
            c = step(lambda e: e.max_index(top_i[:], top[:], logit[:]), c)
            act.wait(c)
            a = act.do(lambda e: e.activation(expl[:], logit[:], ACT.Exp, bias=ntop[:, 0:1],
                                              accum_out=expsum[:, 0:1]), s_ma)
            rt["exp"] = [a]
            c = step(lambda e: e.tensor_copy(top_f[:], top_i[:, 0:1]), c)
            old = tt % 2
            c = step(lambda e: e.tensor_scalar(onehot[:, old, :], ex_iota[:], top_f[:, 0:1], None, ALU.is_equal),
                     c, c_const, *rt.get(("pos", old), []))
            pe.wait(c)
            if tt:
                pe.wait(rt["seen"])
                pe.do(lambda e: e.matmul(p_misc[:, 0:NX], ones_bf[:], seen[:, old, :], start=True, stop=False))
            m = pe.do(lambda e: e.matmul(p_misc[:, 0:NX], tri[:], onehot[:, old, :], start=tt == 0, stop=True), s_pm)
            if tt:
                rt["seen"] = step(lambda e: e.tensor_tensor(seen[:, 1 - old, :], seen[:, old, :], onehot[:, old, :],
                                                            ALU.add), c, *rt.get(("pos", 1 - old), []))
            else:
                rt["seen"] = step(lambda e: e.tensor_copy(seen[:, 1 - old, :], onehot[:, old, :]), c)
            c = step(lambda e: e.tensor_tensor_reduce(pos_junk[:], onehot[:, old, :], p_misc[:, 0:NX], 1.0, 0.0,
                                                      ALU.mult, ALU.add, pos[:, 0:1]), m)
            rt[("pos", old)] = [m]
            misc_free = [c]
            c = step(lambda e: e.tensor_scalar(rej[:], pos[:], float(CAP), FAR, ALU.is_gt, ALU.mult), c)
            c1_ = step(lambda e: e.scalar_tensor_tensor(out=slot_f[:], in0=top_f[:], scalar=float(CAP), in1=pos[:],
                                                        op0=ALU.mult, op1=ALU.add), c)
            c = step(lambda e: e.scalar_tensor_tensor(out=slot_of[:, tt:tt + 1], in0=slot_f[:], scalar=-1.0,
                                                      in1=rej[:], op0=ALU.add, op1=ALU.add), c1_)
            dve.wait(a)
            g = step(lambda e: e.reciprocal(id_gate[:, tt, 1:2], expsum[:]), a)
            pool.wait(c, g, m_tab)
            return pool.do(lambda e: e.indirect_dma_start(
                out=slot_table[:, :], out_offset=bass.IndirectOffsetOnAxis(ap=slot_of[:, tt:tt + 1], axis=0),
                in_=id_gate[:, tt, :], in_offset=None, bounds_check=SLOTS - 1, oob_is_err=False), s_scatter, 16)

        proj_free = [[], []]
        m_q, m_k, m_v = {}, {}, {}

        def project(q, n, f):
            which = (0, 2, 1)[n]
            r = (n * KT + f) % 2
            pe.wait(*m_weights, *[m for t in range(TPQ) for m in m_xparts[q * TPQ + t]], *proj_free[r])
            terms = [(k, a, b) for k in range(KT) for a, b in ((0, 0), (0, 1), (1, 0))]
            for i, (k, a, b) in enumerate(terms):
                m = pe.do(lambda e, i=i, k=k, a=a, b=b: e.matmul(
                    p_proj[:, r, 0:QT], wt[:, which, a, k, f * P:(f + 1) * P], xt[:, b, k, :],
                    start=i == 0, stop=i == len(terms) - 1), s_proj if i == len(terms) - 1 else None)
            last_proj[q] = m
            act.wait(m, m_w[which])
            b = bias[:, which, f:f + 1]
            if which == 2:
                act.wait(*stage_v_free)
                a = act.do(lambda e: e.activation(stage_v[:, f, :], p_proj[:, r, 0:QT], ACT.Identity, bias=b), s_phi)
                proj_free[r] = [a]
            else:
                act.wait(*stage_free)
                hi = stage[:, 0, f, :]
                a = act.do(lambda e: e.activation(hi, p_proj[:, r, 0:QT], ACT.Identity, bias=b), s_phi)
                dve.wait(a)
                d = dve.do(lambda e: e.scalar_tensor_tensor(out=stage[:, 1, f, :], in0=p_proj[:, r, 0:QT], scalar=b,
                                                            in1=hi.bitcast(F32), op0=ALU.add, op1=ALU.subtract),
                           s_plo)
                proj_free[r] = [a, d]
            if f == KT - 1:
                sp.wait(*proj_free[0], *proj_free[1])
                move(q, which)

        stage_free, stage_v_free, q_land_free, v_land_free = [], [], [], []

        def move(q, which):
            if which == 2:
                sp.wait(*v_land_free)
                for c4 in range(4):
                    for g in range(QH):
                        m = sp.do(lambda e, c4=c4, g=g: e.dma_start(
                            v_land[g * D:(g + 1) * D, c4::4, :],
                            stage_v[c4 * D:(c4 + 1) * D, :, g * HT:(g + 1) * HT]), s_v, 16)
                m_v[q] = m
                stage_v_free[:] = [m]
                return
            if which == 0:
                sp.wait(*q_land_free)
            elif q >= 2:
                sp.wait(m_scored[(q - 2) * NT + NT - 1])
            parts = ((0, 1, 0), (0, 0, 1))[which]
            dst, landed = (q_land, s_q) if which == 0 else (ks[q % 2], s_k[q % 2])
            for row, part in enumerate(parts):
                for c4 in range(4):
                    m = sp.do(lambda e, row=row, part=part, c4=c4: e.dma_start(
                        dst[row * D:(row + 1) * D, c4::4, :].bitcast(F32),
                        stage[c4 * D:(c4 + 1) * D, part, :, :].bitcast(F32)), landed, 16)
            (m_q if which == 0 else m_k)[q] = m
            stage_free[:] = [m]

        m_qcopy, m_vcopy, m_scored = {}, {}, {}

        def copy_q(q, j):
            pool.wait(m_q[q])
            if q:
                pool.wait(m_scored[(q - 1) * NT + 2 * j + 1])
            w = 2 * TT
            src = q_land[:].bitcast(F32).rearrange("p c (g t) -> p g t c", g=QH)
            dst = qn[:].rearrange("p (g t) c -> p g t c", g=QH)
            m_qcopy[q, j] = pool.do(lambda e: e.tensor_copy(dst[:, :, j * w:(j + 1) * w, :],
                                                            src[:, :, j * w:(j + 1) * w, :]), s_copy)
            if j == 3:
                q_land_free[:] = [m_qcopy[q, j]]

        def copy_v(q):
            pool.wait(m_v[q])
            if q:
                pool.wait(m_vturned[q - 1])
            m_vcopy[q] = pool.do(lambda e: e.tensor_copy(v_nat[:], v_land[:].rearrange("p c t -> p t c")), s_copy)
            v_land_free[:] = [m_vcopy[q]]

        m_vturned, m_vn, m_far, m_scores_done = {}, {}, {}, {}

        def turn_v(q, half):
            nonlocal misc_free
            par = q % 2
            pe.wait(m_vcopy[q], *misc_free)
            for t in range(4):
                row = (half * 4 + t) * TT
                m = pe.do(lambda e, t=t, row=row: e.transpose(
                    p_misc[:, t * P:(t + 1) * P], v_nat[:, row:row + TT, :].rearrange("p t c -> p (t c)"),
                    ident[:]), s_pm if t == 3 else None)
            m_vturned[q] = m
            act.wait(m)
            if q >= 2:
                act.wait(m_pv[(q - 2) * NT + NT - 1])
            a = act.do(lambda e: e.activation(vn[:, par, half * 4:half * 4 + 4, :].rearrange("p t c -> p (t c)"),
                                              p_misc[:], ACT.Copy), s_ma)
            misc_free = [a]
            m_vn[q] = a

        def far_sums(q):
            nonlocal misc_free
            par = q % 2
            pe.wait(m_vn[q], *misc_free)
            for t in range(NT):
                m = pe.do(lambda e, t=t: e.matmul(p_misc[:, 2 * t:2 * t + 2], vn[:, par, t, :], ones2[:], start=True,
                                                  stop=True), s_pm if t == NT - 1 else None)
            src = p_misc[:, 0:2 * NT].rearrange("p (t two) -> p t two", two=2)[:, :, 0]
            dve.wait(m)
            c = dve.do(lambda e: e.tensor_copy(vsum[:, 0, :], src), s_md)
            dve.wait(c)
            c = dve.do(lambda e: e.tensor_tensor(vsum[:, 1, :], src, vsum[:, 0, :].bitcast(F32), ALU.subtract), s_md)
            pe.wait(c)
            m = pe.do(lambda e: e.transpose(p_misc[0:2 * NT, 0:P],
                                            vsum[:].rearrange("p a t -> p (a t)").bitcast(F32), ident[:]), s_pm)
            act.wait(m)
            a = act.do(lambda e: e.activation(far_rows[:, par, :], p_misc[0:2 * NT, 0:P], ACT.Copy), s_ma)
            misc_free = [a]
            m_far[q] = a

        score_free = [[], []]
        prob_free = [[] for _ in range(SR)]
        prob_free[0] = [m_tab]
        m_exp, m_negm = {}, {}
        m_eout = {}
        m_row_free = {}
        n_score = 0

        def window(T):
            first = max(T - 1, 0)
            return first, min(T + 2, NT) - first

        def scores(s, g):
            nonlocal n_score
            q, T = divmod(s, NT)
            par = q % 2
            first, nj = window(T)
            w = nj * TT
            m_lo = 0 if T else TT
            r = n_score % 2
            slot = n_score % SR
            row = g * HT
            pe.wait(m_qcopy[q, T // 2], m_k[q], *score_free[r])
            m = pe.do(lambda e: e.matmul(
                p_score[:, r, 0:CH * w],
                qn[:, row + T * TT:row + (T + 1) * TT, :].rearrange("p t c -> p (t c)"),
                ks[par][:, :, row + first * TT:row + first * TT + w], start=True, stop=True), s_score)
            m_scored[s] = m
            dve.wait(m, c_const, *prob_free[slot])
            if g == 0 and q >= 2:
                dve.wait(m_row_free[q - 2])
            d = dve.do(lambda e: e.tensor_tensor_reduce(
                prob[:, slot, 0:CH * w].rearrange("p (t c) -> p c t", c=CH),
                p_score[:, r, 0:CH * w].rearrange("p (c t) -> p c t", c=CH),
                mask[:, :, m_lo:m_lo + w], 1.0, 0.0, ALU.mult, ALU.max, row_max[:, par, T, g:g + 1]), s_masked)
            score_free[r] = [d]
            slots_of.setdefault(s, []).append(slot)
            n_score += 1

        slots_of = {}

        def weights(s):
            q, T = divmod(s, NT)
            par = q % 2
            w = window(T)[1] * TT
            masked = slots_of[s]
            dve.wait((s_masked, s_masked.value))
            c = dve.do(lambda e: e.tensor_scalar(neg_max[:, par, T, :], row_max[:, par, T, :], -SCALE, None,
                                                 ALU.mult), s_negm)
            act.wait(c)
            for g, slot in enumerate(masked):
                a = act.do(lambda e, g=g, slot=slot: e.activation(
                    prob[:, slot, 0:CH * w], prob[:, slot, 0:CH * w], ACT.Exp, bias=neg_max[:, par, T, g:g + 1],
                    scale=SCALE, accum_out=row_sum[:, par, T, g:g + 1]), s_exp)
            m_exp[s] = (a, masked)
            m_eout[s] = act.do(lambda e: e.activation(e_out[:, par, T, :], neg_max[:, par, T, :], ACT.Exp), s_exp)

        turn_free = [[], []]
        n_turn = 0
        m_probT, m_pv, turn_step, place_of = {}, {}, {}, {}

        def turn_probs(s, jj):
            nonlocal n_turn
            q, T = divmod(s, NT)
            first, nj = window(T)
            if jj >= nj:
                return
            r = n_turn % 2
            mark, slots = m_exp[s]
            pe.wait(mark, *turn_free[r])
            for g, slot in enumerate(slots):
                m = pe.do(lambda e, g=g, slot=slot: e.transpose(
                    p_turn[:, r, g * P:(g + 1) * P], prob[:, slot, jj * P:(jj + 1) * P], ident[:]),
                    s_turn if g == QH - 1 else None)
            if jj == nj - 1:
                for slot in slots:
                    prob_free[slot] = [m]
            eng, cnt = (act, s_turnedA) if n_turn % 3 == 0 else (dve, s_turnedD)
            eng.wait(m)
            if n_turn >= PR:
                eng.wait(m_pv[turn_step[n_turn - PR]])
            turn_step[n_turn] = s
            dst = probT[:, n_turn % PR, :]
            place_of[s, jj] = n_turn % PR
            if eng is act:
                a = act.do(lambda e: e.activation(dst, p_turn[:, r, :], ACT.Copy), cnt)
            else:
                a = dve.do(lambda e: e.tensor_copy(dst, p_turn[:, r, :]), cnt)
            turn_free[r] = [a]
            m_probT.setdefault(s, []).append(a)
            n_turn += 1

        att_free = []

        def weigh(s):
            q, T = divmod(s, NT)
            par = q % 2
            first, nj = window(T)
            pe.wait(m_vn[q], *m_probT[s], *(att_free if T % 4 == 0 else []))
            col = (T % 4) * P
            for jj in range(nj):
                for g in range(QH):
                    m = pe.do(lambda e, jj=jj, g=g: e.matmul(
                        p_att[g * D:(g + 1) * D, col:col + P], vn[:, par, first + jj, g * D:(g + 1) * D],
                        probT[:, place_of[s, jj], g * P:(g + 1) * P], start=jj == 0, stop=jj == nj - 1,
                        skip_group_check=True), s_pv if jj == nj - 1 and g == QH - 1 else None)
            m_pv[s] = m

        m_addend = {}

        def finish(s):
            nonlocal misc_free, att_free
            q, T = divmod(s, NT)
            half, par = T // 4, q % 2
            t0 = half * 4
            act.wait(m_pv[s])
            if m_addend:
                act.wait(m_addend["attT"])
            a = act.do(lambda e: e.activation(attT[:], p_att[:], ACT.Copy), s_att)
            att_free = [a]
            pe.wait(m_far[q], c_pick, *misc_free)
            for t in range(4):
                m = pe.do(lambda e, t=t: e.matmul(p_misc[:, t * P:(t + 1) * P], far_pick_r[:, t0 + t:t0 + t + 1].broadcast_to([2 * NT, P]),
                                                  far_rows[:, par, :], start=True, stop=True),
                          s_pm if t == 3 else None)
            eo = e_out[:, par, t0:t0 + 4, :].rearrange("p t g -> p (t g)")
            tg = 4 * QH

            def wide(v):
                return v.unsqueeze(2).broadcast_to([P, tg, D])

            def cols(v):
                return v.rearrange("p (n d) -> p n d", d=D)

            dve.wait(m, m_eout[s])
            d = dve.do(lambda e: e.tensor_tensor(cols(far_e[:]), cols(p_misc[:]), wide(eo), ALU.mult), s_post)
            misc_free = [d]
            den_v = den[:, par, t0:t0 + 4, :].rearrange("p t g -> p (t g)")
            rden_v = rden[:, par, t0:t0 + 4, :].rearrange("p t g -> p (t g)")
            c = dve.do(lambda e: e.tensor_tensor(den_v, n_out[:, t0:t0 + 4, :].rearrange("p t g -> p (t g)"), eo,
                                                 ALU.mult), s_post)
            dve.wait(c)
            c = dve.do(lambda e: e.tensor_tensor(den_v, den_v, row_sum[:, par, t0:t0 + 4, :].rearrange(
                "p t g -> p (t g)"), ALU.add), s_post)
            dve.wait(c)
            c = dve.do(lambda e: e.reciprocal(rden_v, den_v), s_post)
            if half == 1:
                m_row_free[q] = c
            pe.wait(a, *misc_free)
            for t in range(4):
                m = pe.do(lambda e, t=t: e.transpose(p_misc[:, t * P:(t + 1) * P], attT[:, t * P:(t + 1) * P],
                                                     ident[:]), s_pm if t == 3 else None)
            m_addend["attT"] = m
            dve.wait(m, d)
            d = dve.do(lambda e: e.tensor_tensor(far_e[:], p_misc[:], far_e[:], ALU.add), s_post)
            misc_free = [d]
            b, qd = divmod(q, QB)
            dve.wait(d, c)
            if qd == 0:
                for t in range(4):
                    dve.wait(*ao_free[t0 + t])
            for_t = ao[:, t0:t0 + 4, qd * P:(qd + 1) * P].rearrange("p t (g d) -> p t g d", d=D)
            tiles = far_e[:].rearrange("p (t g d) -> p t g d", t=4, g=QH)
            rd = rden[:, par, t0:t0 + 4, :]
            for t in range(4):
                d = dve.do(lambda e, t=t: e.tensor_tensor(
                    for_t[:, t], tiles[:, t], rd[:, t].unsqueeze(2).broadcast_to([P, QH, D]), ALU.mult), s_post)
            m_addend["far_e"] = d
            if qd == QB - 1:
                for t in range(4):
                    T_, tt = t0 + t, b * NT + t0 + t
                    sp.wait(m_sum[tt], *late_free)
                    m = sp.do(lambda e, tt=tt: e.dma_start(late[:], sum_rows[tt * P:(tt + 1) * P, :]), s_late, 16)
                    pool.wait(m, d)
                    m = pool.do(lambda e, T_=T_: e.tensor_tensor(ao[:, T_, :], ao[:, T_, :], late[:], ALU.add),
                                s_resdone)
                    late_free[:] = [m]
                    sp.wait(m)
                    m1 = sp.do(lambda e, tt=tt, T_=T_: e.dma_start(out_rows[tt * P:(tt + 1) * P, :], ao[:, T_, :]),
                               s_store[T_], 16)
                    m2 = sp.do(lambda e, tt=tt, T_=T_: e.dma_start(base_rows[tt * P:(tt + 1) * P, :], ao[:, T_, :]),
                               s_base[T_], 16)
                    ao_free[T_] = [m1, m2]

        for tt in range(TPQ):
            load_x(tt)
        norm_scale(0)
        for tt in range(TPQ):
            layer_norm(tt)
            turn_x(tt)
            load_x(tt + TPQ)
        norm_scale(1)
        for f in range(3 * KT):
            project(0, f // KT, f % KT)
        for tt in range(TPQ):
            route(tt)
        for j in range(4):
            copy_q(0, j)
        copy_v(0)
        for tt in range(TPQ, 2 * TPQ):
            layer_norm(tt)
            turn_x(tt)
            route(tt)
            load_x(tt + TPQ)
        NS = NQ * NT
        CHUNKS = [(0, 1), (2,), (3, 4), (5,), (6, 7), (8, 9), (10, 11), ()]
        for g in range(QH):
            scores(0, g)
        weights(0)
        for s in range(NS + 3):
            q, T = divmod(s, NT)
            if s + 1 < NS:
                scores(s + 1, 0)
                scores(s + 1, 1)
            if T == 0 and q < NQ:
                turn_v(q, 0)
            if q + 1 < NQ:
                for f in CHUNKS[T]:
                    project(q + 1, f // KT, f % KT)
            if s + 1 < NS:
                scores(s + 1, 2)
                scores(s + 1, 3)
                weights(s + 1)
            if s < NS:
                turn_probs(s, 0)
            if T == 0 and q < NQ:
                turn_v(q, 1)
            if T == 1 and q < NQ:
                far_sums(q)
            if 1 <= s <= NS:
                weigh(s - 1)
            if s < NS:
                turn_probs(s, 1)
            if 1 <= s <= NS and (s - 1) % 4 == 3:
                finish(s - 1)
            if s < NS:
                turn_probs(s, 2)
            if q + 2 < NQ:
                if T == 2:
                    norm_scale(q + 2)
                if T in (3, 4):
                    layer_norm((q + 2) * TPQ + T - 3)
                if T == 7:
                    for tt in range((q + 2) * TPQ, (q + 3) * TPQ):
                        turn_x(tt)
                        route(tt)
            if q + 1 < NQ:
                if T == 5:
                    for j in range(3):
                        copy_q(q + 1, j)
                    copy_v(q + 1)
                if T == 7:
                    copy_q(q + 1, 3)
            if T in (5, 6) and q + 3 < NQ:
                load_x((q + 3) * TPQ + T - 5)

        end1 = [(c, c.value) for c in (
            s_const, s_scatter, s_ln, s_newton, s_resadd, s_xturn, s_xhi, s_xlo, s_proj, s_phi, s_plo, s_score, s_masked,
            s_negm, s_exp, s_turn, s_turnedA, s_turnedD, s_pv, s_att, s_post, s_pm, s_ma, s_md, s_rt, s_resdone,
            s_load, s_pw, s_aw, s_dw, s_tab, *s_store, *s_base, *s_sum, s_late, *s_xnst, *s_x, s_q, *s_k, s_v, s_copy, *s_wraw) if c.value]
        c1.close()

        RW = 4
        RS = 4
        NR = -(-CAP // P)
        wide_of = [min(P, CAP - r * P) for r in range(NR)]
        tab_rows = sb("tab_rows", [NX, 2 * CAP])
        token_of = sb("token_of", [P, NR, NX], U32)
        gate_of = sb("gate_of", [P, NR, NX])
        xg = sb("xg", [P, 2, NR, E])
        yb = sb("yb", [P, 2, NR, E])
        xe = sb("xe", [P, 2, 2, KT, CAP], F32R)
        wraw = sb("wraw", [P, RW, KT, FF])
        wsplit = sb("wsplit", [P, RS, 2, KT, FF], F32R)
        eg = sb("eg", [P, 2, CAP])
        sg = sb("sg", [P, 2, CAP])
        hid = sb("hid", [P, 2, CAP])
        hparts = sb("hparts", [P, 2, KT, CAP], F32R)

        s_tabin = sem("s_tabin")
        s_pt = sem("s_pt")
        s_at = sem("s_at")
        s_dt = sem("s_dt")
        s_clear = sem("s_clear")
        s_wr = [sem(f"s_wr{i}") for i in range(RW)]
        s_whi = sem("s_whi")
        s_wloD = sem("s_wlo_dve")
        s_wloP = sem("s_wlo_pool")
        s_xg = [sem(f"s_xg{i}") for i in range(2)]
        s_yb = [sem(f"s_yb{i}") for i in range(2)]
        s_ys = [sem(f"s_ys{i}") for i in range(2)]
        s_xeP = sem("s_xe_pe")
        s_xeA = sem("s_xe_act")
        s_xeD = sem("s_xe_dve")
        s_gu = sem("s_gu")
        s_eg = sem("s_eg")
        s_sg = sem("s_sg")
        s_hid = sem("s_hid")
        s_hhi = sem("s_hhi")
        s_hlo = sem("s_hlo")
        s_down = sem("s_down")
        s_y = sem("s_y")

        for eng in (pe, act, dve, pool, sp):
            eng.wait(*end1)

        m_tabin = sp.do(lambda e: e.dma_start(tab_rows[:], slot_table.rearrange("(n c) two -> n (c two)", n=NX)),
                        s_tabin, 16)
        c_clear = dve.do(lambda e: e.memset(xg[:], 0.0), s_clear)
        c_clear = dve.do(lambda e: e.memset(yb[:], 0.0), s_clear)
        pe.wait(m_tabin)
        rows = tab_rows[:].rearrange("n (c two) -> n c two", two=2)
        for r in range(NR):
            for v in range(2):
                m = pe.do(lambda e, r=r, v=v: e.transpose(
                    p_misc[0:wide_of[r], (2 * r + v) * NX:(2 * r + v + 1) * NX],
                    rows[:, r * P:r * P + wide_of[r], v], ident[0:NX, 0:NX]), s_pt)
        dve.wait(m)
        for r in range(NR):
            w = wide_of[r]
            dve.do(lambda e, r=r, w=w: e.tensor_copy(token_of[0:w, r, :], p_misc[0:w, 2 * r * NX:(2 * r + 1) * NX]),
                   s_dt)
            c_tab = dve.do(lambda e, r=r, w=w: e.tensor_copy(gate_of[0:w, r, :],
                                                             p_misc[0:w, (2 * r + 1) * NX:(2 * r + 2) * NX]), s_dt)

        m_wr2, m_wsplit, m_used = {}, {}, {}

        def load_w(i):
            x_, which = divmod(i, 3)
            src = (w_gate, w_up, w_down)[which]
            if i >= RW:
                sp.wait(*m_wsplit[i - RW])
            m_wr2[i] = sp.do(lambda e: e.dma_start(wraw[:, i % RW], src[x_].rearrange("(k p) f -> p k f", p=P)),
                             s_wr[i % RW], 16)

        def split_w(i):
            r, t = i % RW, i % RS
            act.wait(m_wr2[i])
            if i >= RS:
                act.wait(m_used[i - RS])
            a = act.do(lambda e: e.activation(wsplit[:, t, 0], wraw[:, r], ACT.Copy), s_whi)
            eng, cnt = (pool, s_wloP) if i % 3 == 2 else (dve, s_wloD)
            eng.wait(a)
            d = eng.do(lambda e: e.tensor_tensor(wsplit[:, t, 1], wraw[:, r], wsplit[:, t, 0].bitcast(F32),
                                                 ALU.subtract), cnt)
            m_wsplit[i] = [a, d]

        m_xg, m_yb, m_xeturn, m_ys, m_xe = {}, {}, {}, {}, {}

        def gather(x_):
            p2 = x_ % 2
            pool.wait(c_tab, c_clear)
            if x_ >= 2:
                pool.wait(m_xeturn[x_ - 2], m_ys[x_ - 2])
            for dst, src, cnt, marks in ((xg, xn_rows, s_xg, m_xg), (yb, base_rows, s_yb, m_yb)):
                for r in range(NR):
                    w = wide_of[r]
                    marks[x_] = pool.do(lambda e, r=r, w=w, dst=dst, src=src: e.indirect_dma_start(
                        out=dst[0:w, p2, r, :], out_offset=None, in_=src[:, :],
                        in_offset=bass.IndirectOffsetOnAxis(ap=token_of[0:w, r, x_:x_ + 1], axis=0),
                        bounds_check=TOK - 1, oob_is_err=False), cnt[p2], 16)

        xe_free = [[], []]
        xbank = [p_misc[:], p_proj[:, 0, :]]
        n_x = 0

        def turn_xe(x_):
            nonlocal n_x
            p2 = x_ % 2
            m_xe[x_] = []
            pe.wait(m_xg[x_])
            for r in range(NR):
                w = wide_of[r]
                bank = xbank[n_x % 2]
                pe.wait(*xe_free[n_x % 2])
                for k in range(KT):
                    m = pe.do(lambda e, r=r, w=w, k=k, bank=bank: e.transpose(
                        bank[:, k * w:(k + 1) * w], xg[0:w, p2, r, k * P:(k + 1) * P], ident[0:w, 0:w]),
                        s_xeP if k == KT - 1 else None)
                src = bank[:, 0:KT * w].rearrange("p (k t) -> p k t", k=KT)
                act.wait(m)
                if x_ >= 2:
                    act.wait(m_gu_last[x_ - 2])
                hi = xe[:, p2, 0, :, r * P:r * P + w]
                lo = xe[:, p2, 1, :, r * P:r * P + w]
                a = act.do(lambda e, hi=hi, src=src: e.activation(hi, src, ACT.Copy), s_xeA)
                dve.wait(a)
                d = dve.do(lambda e, hi=hi, lo=lo, src=src: e.tensor_tensor(lo, src, hi.bitcast(F32), ALU.subtract),
                           s_xeD)
                xe_free[n_x % 2] = [a, d]
                m_xe[x_] += [a, d]
                n_x += 1
            m_xeturn[x_] = m

        m_gu_last, m_h = {}, {}
        gu_free = [[c_tab], []]
        h_free = []
        PARTS = ((0, 0), (0, 1), (1, 0))

        def gate_up(x_, f):
            n = x_ * KT + f
            r, p2 = n % 2, x_ % 2
            for which, bank in ((0, p_score), (1, p_turn)):
                i = 3 * x_ + which
                pe.wait(*m_wsplit[i], *m_xe[x_], *gu_free[r])
                terms = [(k, a, b) for k in range(KT) for a, b in PARTS]
                for j, (k, a, b) in enumerate(terms):
                    m = pe.do(lambda e, j=j, k=k, a=a, b=b, bank=bank, i=i: e.matmul(
                        bank[:, r, 0:CAP], wsplit[:, i % RS, a, k, f * P:(f + 1) * P], xe[:, p2, b, k, :],
                        start=j == 0, stop=j == len(terms) - 1), s_gu if j == len(terms) - 1 else None)
                m_used[i] = m
                if which == 0:
                    m_g = m
            m_gu_last[x_] = m
            g_, u_ = p_score[:, r, 0:CAP], p_turn[:, r, 0:CAP]
            act.wait(m_g)
            if n >= 2:
                act.wait(sg_marks[n - 2])
            a = act.do(lambda e: e.activation(eg[:, r], g_, ACT.Exp, scale=-1.0), s_eg)
            act.wait(a)
            a = act.do(lambda e: e.activation(eg[:, r], eg[:, r], ACT.Identity, bias=1.0), s_eg)
            dve.wait(a)
            c = dve.do(lambda e: e.reciprocal(sg[:, r], eg[:, r]), s_sg)
            sg_marks[n] = c
            dve.wait(c)
            c = dve.do(lambda e: e.tensor_tensor(sg[:, r], sg[:, r], g_, ALU.mult), s_sg)
            dve.wait(c, m)
            if n >= 2:
                dve.wait(m_h[n - 2][0])
            c = dve.do(lambda e: e.tensor_tensor(hid[:, r], sg[:, r], u_, ALU.mult), s_hid)
            gu_free[r] = [c]
            act.wait(c, *h_free)
            a = act.do(lambda e: e.activation(hparts[:, 0, f, :], hid[:, r], ACT.Copy), s_hhi)
            dve.wait(a)
            d = dve.do(lambda e: e.tensor_tensor(hparts[:, 1, f, :], hid[:, r], hparts[:, 0, f, :].bitcast(F32),
                                                 ALU.subtract), s_hlo)
            m_h[n] = [a, d]

        sg_marks = {}
        y_free = [[], []]
        ybank = [p_proj[:, 1, :], p_att[:]]
        n_y = 0

        def down(x_):
            nonlocal n_y, h_free
            p2, i = x_ % 2, 3 * x_ + 2
            last = []
            for r in range(NR):
                w = wide_of[r]
                b2 = n_y % 2
                pe.wait(*m_wsplit[i], *y_free[b2])
                terms = [(f, a, b) for f in range(KT) for a, b in PARTS]
                for j, (f, a, b) in enumerate(terms):
                    pe.wait(*m_h[x_ * KT + f])
                    m = pe.do(lambda e, j=j, f=f, a=a, b=b, w=w, b2=b2, r=r: e.matmul(
                        ybank[b2][0:w, :], hparts[:, a, f, r * P:r * P + w], wsplit[:, i % RS, b, f, :],
                        start=j == 0, stop=j == len(terms) - 1), s_down if j == len(terms) - 1 else None)
                dve.wait(m, m_yb[x_])
                d = dve.do(lambda e, w=w, b2=b2, r=r: e.scalar_tensor_tensor(
                    out=yb[0:w, p2, r, :], in0=ybank[b2][0:w, :], scalar=gate_of[0:w, r, x_:x_ + 1],
                    in1=yb[0:w, p2, r, :], op0=ALU.mult, op1=ALU.add), s_y)
                y_free[b2] = [d]
                last.append(d)
                n_y += 1
            m_used[i] = m
            h_free = [m]
            pend.append((x_, last))

        pend = []

        def scatter(x_, last):
            p2 = x_ % 2
            for r in range(NR):
                w = wide_of[r]
                pool.wait(last[r])
                m_ys[x_] = pool.do(lambda e, r=r, w=w: e.indirect_dma_start(
                    out=out_rows[:, :], out_offset=bass.IndirectOffsetOnAxis(ap=token_of[0:w, r, x_:x_ + 1], axis=0),
                    in_=yb[0:w, p2, r, :], in_offset=None, bounds_check=TOK - 1, oob_is_err=False), s_ys[p2], 16)

        for i in range(RW):
            load_w(i)
        gather(0)
        gather(1)
        turn_xe(0)
        for i in range(3):
            split_w(i)
            load_w(i + RW)
        for x_ in range(NX):
            for f in range(KT):
                gate_up(x_, f)
                i = 3 * (x_ + 1) + f
                if f < 1 and x_ + 1 < NX:
                    split_w(i)
                    if i + RW < 3 * NX:
                        load_w(i + RW)
            if x_ + 1 < NX:
                turn_xe(x_ + 1)
            down(x_)
            scatter(*pend.pop())
            if x_ + 2 < NX:
                gather(x_ + 2)
            for f in (1, 2):
                i = 3 * (x_ + 1) + f
                if x_ + 1 < NX:
                    split_w(i)
                    if i + RW < 3 * NX:
                        load_w(i + RW)

        sp.wait(*[(c, c.value) for c in s_ys])

        block = ctx.enter_context(nc.Block())

        @block.tensor
        def _(e):
            pe.play(e)

        @block.scalar
        def _(e):
            act.play(e)

        @block.vector
        def _(e):
            dve.play(e)

        @block.gpsimd
        def _(e):
            pool.play(e)

        @block.sync
        def _(e):
            sp.play(e)


_INS = ["L0_attn_x", "L0_attn_Wq", "L0_attn_bq", "L0_attn_Wk", "L0_attn_bk", "L0_attn_Wv", "L0_attn_bv",
        "L0_ffn_w_router", "L0_ffn_w_gate", "L0_ffn_w_up", "L0_ffn_w_down"]


def kernel(**inputs):
    import concourse.bacc as bacc
    from concourse.bass_utils import run_bass_kernel_spmd

    nc = bacc.Bacc("TRN2", target_bir_lowering=False, num_devices=1)
    arrays, args = {}, []
    for name in _INS:
        a = np.ascontiguousarray(inputs[name])
        arrays[f"in_{name}"] = a
        args.append(nc.dram_tensor(f"in_{name}", a.shape, mybir.dt.from_np(a.dtype), kind="ExternalInput").ap())
    shape = inputs["L0_attn_x"].shape
    out = nc.dram_tensor("out_x", shape, F32, kind="ExternalOutput").ap()
    build(nc, *args, out)
    r = run_bass_kernel_spmd(nc, [arrays], core_ids=[0])
    return r.results[0]["out_x"]
```

```python
from contextlib import ExitStack

import numpy as np
import concourse.bass as bass
from concourse import mybir

ALU = mybir.AluOpType
ACT = mybir.ActivationFunctionType
F32 = mybir.dt.float32
F32R = mybir.dt.float32r
BF16 = mybir.dt.bfloat16
U32 = mybir.dt.uint32
I32 = mybir.dt.int32
AX = mybir.AxisListType

P = 128


class Counter:

    def __init__(self, handle):
        self.handle = handle
        self.value = 0


class Queue:

    def __init__(self):
        self.steps = []
        self.waited = {}

    def wait(self, *marks):
        for counter, value in marks:
            if self.waited.get(counter, 0) < value:
                self.waited[counter] = value
                self.steps.append((counter.handle, value))

    def do(self, emit, counter=None, by=1):
        if counter is None:
            self.steps.append((emit,))
            return None
        counter.value += by
        self.steps.append((emit, counter.handle, by))
        return (counter, counter.value)

    def play(self, engine):
        for step in self.steps:
            if len(step) == 2:
                engine.wait_ge(step[0], step[1])
            elif len(step) == 1:
                step[0](engine)
            else:
                step[0](engine).then_inc(step[1], step[2])


def build(nc, x, Wq, bq, Wk, bk, Wv, bv, w_router, w_gate, w_up, w_down, out):
    B, S, E = x.shape
    H = 16
    D = E // H
    CH = E // D
    HT = S // CH
    BAND = 128
    TOK = B * S
    NX, _, FF = w_gate.shape
    CAP = -(-5 * TOK // (4 * NX))
    SLOTS = NX * CAP
    KT = E // P
    QH = 4
    QT = QH * HT
    NQ = TOK // QT
    QB = H // QH
    NT = S // P
    TT = P // CH
    TPQ = QT // P
    XR = 2
    PR = 6
    SR = 8
    LR = 1 + TPQ
    NR = -(-CAP // P)
    wide_of = [min(P, CAP - r * P) for r in range(NR)]
    SCALE = float(D) ** -0.5
    FAR = float(1 << 20)
    assert BAND == P and QT == 256 and TT == 8 and FF == E and E == 512

    Q = {n: Queue() for n in ("pe", "act", "dve", "pool", "sp")}
    pe, act, dve, pool, sp = (Q[n] for n in ("pe", "act", "dve", "pool", "sp"))

    x_rows = x.rearrange("b s e -> (b s) e")
    out_rows = out.rearrange("b s e -> (b s) e")
    xn_rows = nc.dram_tensor("xn_rows", [TOK, E], F32, kind="Internal").ap()
    sum_rows = nc.dram_tensor("sum_rows", [TOK, E], F32, kind="Internal").ap()
    base_rows = nc.dram_tensor("base_rows", [TOK, E], F32, kind="Internal").ap()
    v_rows = nc.dram_tensor("v_rows", [TOK, E], F32, kind="Internal").ap()
    slot_table = nc.dram_tensor("slot_table", [SLOTS, 2], F32, kind="Internal").ap()

    with ExitStack() as ctx:
        def sem(name):
            return Counter(ctx.enter_context(nc.semaphore(name)))

        def sb(name, shape, dt=F32, c=None):
            return (c or ctx).enter_context(nc.sbuf_tensor(name, shape, dt))

        def ps(name, shape):
            return ctx.enter_context(nc.psum_tensor(name, shape, F32))

        p_score = ps("p_score", [P, 2, 512])
        p_turn = ps("p_turn", [P, 2, 512])
        p_att = ps("p_att", [P, 512])
        p_proj = ps("p_proj", [P, 2, 512])
        p_misc = ps("p_misc", [P, 512])

        token_of = sb("token_of", [P, NR, NX], U32)
        gate_of = sb("gate_of", [P, NR, NX])
        ident = sb("ident", [P, P])
        slot_of = sb("slot_of", [P, TOK // P], U32)
        id_gate = sb("id_gate", [P, TOK // P, 2])

        s_const = sem("s_const")
        s_scatter = sem("s_scatter")
        s_tabin = sem("s_tabin")
        s_dt = sem("s_dt")
        s_store = [sem(f"s_store{i}") for i in range(NT)]
        s_base = [sem(f"s_base{i}") for i in range(NT)]
        s_sum = [sem(f"s_sum{i}") for i in range(XR)]
        s_xnst = [sem(f"s_xnst{i}") for i in range(TPQ)]

        c1 = ctx.enter_context(ExitStack())

        def sb1(name, shape, dt=F32):
            return sb(name, shape, dt, c1)

        wt = sb1("wt", [P, 3, 2, KT, E], F32R)
        bias = sb1("bias", [P, 3, KT])
        wr = sb1("wr", [P, KT, NX])
        wr_parts = sb1("wr_parts", [P, KT, 2, NX], F32R)
        mask = sb1("mask", [P, CH, 3 * TT])
        q_land = sb1("q_land", [96, CH, QT], F32R)
        qn = sb1("qn", [96, QT, CH], F32R)
        ks = [sb1(f"ks{i}", [96, CH, QT], F32R) for i in range(2)]
        stage = sb1("stage", [P, 2, KT, QT], F32R)
        bias_v = sb1("bias_v", [P, E])
        xt = sb1("xt", [P, 2, KT, QT], F32R)
        xn = sb1("xn", [P, TPQ, E])
        res = sb1("res", [P, XR, E])
        prob = sb1("prob", [P, SR, 3 * P])
        row_max = sb1("row_max", [P, 2, NT, QH])
        vsum = sb1("vsum", [P, 2, NT], F32R)
        far_pick = sb1("far_pick", [2 * NT, NT])
        ones2 = sb1("ones2", [P, 2])
        stats = sb1("stats", [P, TPQ, 6])
        moments = sb1("moments", [P, TPQ, 2])
        rstd = sb1("rstd", [P, TPQ])
        veps = sb1("veps", [P, TPQ])
        newton = sb1("newton", [P, TPQ])
        tri = sb1("tri", [P, P], BF16)
        ones_bf = sb1("ones_bf", [P, P], BF16)
        ex_iota = sb1("ex_iota", [P, NX])
        logitT = sb1("logitT", [2 * NX, QT])
        logit = sb1("logit", [P, TPQ, NX])
        logit_lo = sb1("logit_lo", [P, TPQ, NX])
        top = sb1("top", [P, TPQ, 8])
        top_i = sb1("top_i", [P, TPQ, 8], U32)
        top_f = sb1("top_f", [P, TPQ])
        ntop = sb1("ntop", [P, TPQ])
        expl = sb1("expl", [P, TPQ, NX])
        expsum = sb1("expsum", [P, TPQ])
        onehot = sb1("onehot", [P, 2, NX], BF16)
        seen = sb1("seen", [P, 2, NX], BF16)
        pos_junk = sb1("pos_junk", [P, TPQ, NX])
        pos = sb1("pos", [P, TPQ])
        rej = sb1("rej", [P, TPQ])
        slot_f = sb1("slot_f", [P, TPQ])
        probT = sb1("probT", [P, PR, QH * P])
        vn = sb1("vn", [P, 2, NT, P])
        attT = sb1("attT", [P, 4 * P])
        far_e = sb1("far_e", [P, 4 * P])
        neg_max = sb1("neg_max", [P, 2, NT, QH])
        e_out = sb1("e_out", [P, 2, NT, QH])
        row_sum = sb1("row_sum", [P, 2, NT, QH])
        den = sb1("den", [P, 2, NT, QH])
        rden = sb1("rden", [P, 2, NT, QH])
        n_out = sb1("n_out", [P, NT, QH])
        far_rows = sb1("far_rows", [2 * NT, 2, P], F32R)
        far_pick_r = sb1("far_pick_r", [2 * NT, NT], F32R)
        ao = sb1("ao", [P, NT, E])
        late = sb1("late", [P, E])
        stage_v = sb1("stage_v", [P, TPQ, E])

        s_load = sem("s_load")
        s_bv = sem("s_bv")
        s_wraw = [sem(f"s_wraw{i}") for i in range(3)]
        s_pw = sem("s_pw")
        s_aw = sem("s_aw")
        s_dw = sem("s_dw")
        s_tab = sem("s_tab")

        def fill(t, v):
            return pool.do(lambda e: e.memset(t, v), s_const)

        fill(ident[:], 0.0)
        c0 = fill(mask[:], 1.0)
        pool.wait(c0)
        pool.do(lambda e: e.affine_select(out=ident[:], in_=ident[:], compare_op=ALU.not_equal, fill=1.0, base=0,
                                          pattern=[[-1, P]], channel_multiplier=1), s_const)
        c0 = pool.do(lambda e: e.affine_select(out=mask[:], in_=mask[:], compare_op=ALU.is_ge, fill=0.0, base=0,
                                               pattern=[[1, CH], [CH, 3 * TT]], channel_multiplier=-1), s_const)
        pool.wait(c0)
        pool.do(lambda e: e.affine_select(out=mask[:], in_=mask[:], compare_op=ALU.is_gt, fill=0.0, base=2 * BAND,
                                          pattern=[[-1, CH], [-CH, 3 * TT]], channel_multiplier=1), s_const)
        fill(ones2[:], 1.0)
        fill(ones_bf[:], 1.0)
        c0 = fill(tri[:], 1.0)
        pool.wait(c0)
        pool.do(lambda e: e.affine_select(out=tri[:], in_=tri[:], compare_op=ALU.is_ge, fill=0.0, base=0,
                                          pattern=[[1, P]], channel_multiplier=-1), s_const)
        pool.do(lambda e: e.iota(ex_iota[:], pattern=[[1, NX]], base=0, channel_multiplier=0,
                                 allow_small_or_imprecise_dtypes=True), s_const)
        pool.do(lambda e: e.iota(id_gate[:, :, 0], pattern=[[P, TOK // P]], base=0, channel_multiplier=1,
                                 allow_small_or_imprecise_dtypes=True), s_const)
        c0 = fill(n_out[:], float(S - 3 * P))
        pool.wait(c0)
        fill(n_out[:, 0, :], float(S - 2 * P))
        fill(n_out[:, NT - 1, :], float(S - 2 * P))
        c0 = fill(far_pick[:], 1.0)

        def pick(base, step, fill_value):
            nonlocal c0
            pool.wait(c0)
            c0 = pool.do(lambda e: e.affine_select(out=far_pick[:], in_=far_pick[:], compare_op=ALU.not_equal,
                                                   fill=fill_value, base=base, pattern=[[step, NT]],
                                                   channel_multiplier=-1), s_const)

        for off in (-1, 0, 1, NT - 1, NT, NT + 1):
            pick(off, 1, 0.0)
        pick(NT - 1, -1000, 1.0)
        pick(NT + 1000 * (NT - 1), -1000, 1.0)
        table_init = prob[:, 0, 0:2 * SLOTS // P].rearrange("p (n two) -> p n two", two=2)
        fill(table_init[:, :, 0], FAR)
        c_const = fill(table_init[:, :, 1], 0.0)
        sp.wait(c_const)
        m_tab = sp.do(lambda e: e.dma_start(slot_table.rearrange("(p n) two -> p (n two)", p=P),
                                            prob[:, 0, 0:2 * SLOTS // P]), s_tab, 16)
        dve.wait(c_const)
        c_pick = dve.do(lambda e: e.tensor_copy(far_pick_r[:], far_pick[:]), s_dw)

        raw = [vn[:].rearrange("p a t c -> p (a t c)"), ao[:, 0:4, :].rearrange("p t e -> p (t e)"),
               ao[:, 4:8, :].rearrange("p t e -> p (t e)")]
        m_w = []
        for i, (w, b) in enumerate(((Wq, bq), (Wk, bk), (Wv, bv))):
            dst = raw[i].rearrange("p (t e) -> p t e", t=KT)
            sp.do(lambda e, dst=dst, w=w: e.dma_start(dst, w.rearrange("(t p) e -> p t e", p=P)), s_wraw[i], 16)
            m_w.append(sp.do(lambda e, i=i, b=b: e.dma_start(bias[:, i, :], b.rearrange("(t p) -> p t", p=P), allow_slow_non_contiguous=True),
                             s_wraw[i], 16))
        m_bv = sp.do(lambda e: e.dma_start(bias_v[:], bv.unsqueeze(0).broadcast_to([P, E])), s_bv, 16)
        m_wr = sp.do(lambda e: e.dma_start(wr[:], w_router.rearrange("(k p) n -> p k n", p=P)), s_load, 16)
        dve.wait(m_wr)
        c0 = dve.do(lambda e: e.tensor_copy(wr_parts[:, :, 0, :], wr[:]), s_dw)
        dve.wait(c0)
        m_wrp = dve.do(lambda e: e.tensor_tensor(wr_parts[:, :, 1, :], wr[:], wr_parts[:, :, 0, :].bitcast(F32), ALU.subtract),
                       s_dw)

        pe.wait(c_const)
        free = [[], []]
        for i in range(3):
            pe.wait(m_w[i])
            src = raw[i].rearrange("p (t e) -> p t e", t=KT)
            for k in range(KT):
                r = (i * KT + k) % 2
                pe.wait(*free[r])
                for f in range(KT):
                    m = pe.do(lambda e, r=r, f=f, k=k, src=src: e.transpose(
                        p_turn[:, r, f * P:(f + 1) * P], src[:, f, k * P:(k + 1) * P], ident[:]),
                        s_pw if f == KT - 1 else None)
                act.wait(m)
                a = act.do(lambda e, r=r, i=i, k=k: e.activation(wt[:, i, 0, k, :], p_turn[:, r, :], ACT.Copy), s_aw)
                dve.wait(m, a)
                d = dve.do(lambda e, r=r, i=i, k=k: e.tensor_tensor(
                    wt[:, i, 1, k, :], p_turn[:, r, :], wt[:, i, 0, k, :].bitcast(F32), ALU.subtract), s_dw)
                free[r] = [a, d]
        m_weights = free[0] + free[1]

        s_x = [sem(f"s_x{i}") for i in range(XR)]
        s_q = [sem(f"s_q{i}") for i in range(3)]
        s_k = [[sem(f"s_k{i}{j}") for j in range(3)] for i in range(2)]
        s_vst = sem("s_vst")
        s_v = [sem(f"s_v{i}") for i in range(2)]
        s_copy = sem("s_copy")
        s_ln = sem("s_ln")
        s_newton = sem("s_newton")
        s_resadd = sem("s_resadd")
        s_xturn = sem("s_xturn")
        s_xhi = sem("s_xhi")
        s_xlo = sem("s_xlo")
        s_proj = sem("s_proj")
        s_phi = sem("s_phi")
        s_plo = sem("s_plo")
        s_score = sem("s_score")
        s_masked = sem("s_masked")
        s_negm = sem("s_negm")
        s_exp = sem("s_exp")
        s_turn = sem("s_turn")
        s_turnedA = sem("s_turned_act")
        s_turnedD = sem("s_turned_dve")
        s_pv = sem("s_pv")
        s_att = sem("s_att")
        s_post = sem("s_post")
        s_norm = sem("s_norm")
        s_pm = sem("s_pm")
        s_ma = sem("s_ma")
        s_md = sem("s_md")
        s_rt = sem("s_rt")
        s_resdone = sem("s_resdone")
        s_late = [sem(f"s_late{i}") for i in range(LR)]

        misc_free = []
        res_free = [[] for _ in range(XR)]
        ao_free = [m_weights] * NT
        late_free = [[] for _ in range(LR)]
        m_x, m_ln, m_xadd, m_xnst, m_sum, m_rstd = {}, {}, {}, {}, {}, {}

        def load_x(tt):
            sp.wait(*res_free[tt % XR])
            m_x[tt] = sp.do(lambda e: e.dma_start(res[:, tt % XR, :], x_rows[tt * P:(tt + 1) * P, :]),
                            s_x[tt % XR], 16)

        def norm_stats(tt):
            j, r = tt % TPQ, tt % XR
            dve.wait(m_x[tt])
            if tt >= TPQ:
                dve.wait(m_ln[tt - TPQ])
            c = dve.do(lambda e: e.bn_stats(stats[:, j, :], res[:, r, :]), s_ln)
            dve.wait(c)
            m_moments[tt] = dve.do(lambda e: e.bn_aggr(moments[:, j, :], stats[:, j, :]), s_ln)

        m_moments = {}

        def norm_scale(q):
            dve.wait(*[m_moments[q * TPQ + t] for t in range(TPQ)])
            if q:
                dve.wait(m_rstd[q - 1])
            c = dve.do(lambda e: e.tensor_scalar(veps[:], moments[:, :, 1], 1e-5, None, ALU.add), s_ln)
            dve.wait(c)
            if q:
                dve.wait(m_ln[q * TPQ - 1])
            c = dve.do(lambda e: e.tensor_scalar(rstd[:].bitcast(I32), veps[:].bitcast(I32), -0.5,
                                                 float(0x5F3759DF), ALU.mult, ALU.add), s_ln)

            def step(emit):
                nonlocal c
                pool.wait(c)
                c = pool.do(emit, s_newton)

            for _ in range(3):
                step(lambda e: e.tensor_tensor(newton[:], rstd[:], rstd[:], ALU.mult))
                step(lambda e: e.tensor_tensor(newton[:], newton[:], veps[:], ALU.mult))
                step(lambda e: e.tensor_scalar(newton[:], newton[:], -0.5, 1.5, ALU.mult, ALU.add))
                step(lambda e: e.tensor_tensor(rstd[:], rstd[:], newton[:], ALU.mult))
            m_rstd[q] = c

        def layer_norm(tt):
            j, r = tt % TPQ, tt % XR
            dve.wait(m_rstd[tt // TPQ])
            if tt >= TPQ:
                dve.wait(m_xturn[tt - TPQ], m_xnst[tt - TPQ], m_xadd[tt - TPQ])
            m_ln[tt] = dve.do(lambda e: e.tensor_scalar(xn[:, j, :], res[:, r, :], moments[:, j, 0:1],
                                                        rstd[:, j:j + 1], ALU.subtract, ALU.mult), s_ln)
            pool.wait(m_ln[tt])
            m_xadd[tt] = pool.do(lambda e: e.tensor_tensor(res[:, r, :], res[:, r, :], xn[:, j, :], ALU.add),
                                 s_resadd)
            sp.wait(m_ln[tt])
            sp.wait(m_xadd[tt])
            m_sum[tt] = sp.do(lambda e: e.dma_start(sum_rows[tt * P:(tt + 1) * P, :], res[:, r, :]), s_sum[r], 16)
            res_free[r] = [m_sum[tt]]
            m_xnst[tt] = sp.do(lambda e: e.dma_start(xn_rows[tt * P:(tt + 1) * P, :], xn[:, j, :]), s_xnst[j], 16)

        m_xturn, m_xparts = {}, {}
        proj_free = [[], []]
        n_proj = 0

        def turn_x(tt):
            nonlocal n_proj
            j = tt % TPQ
            bank = n_proj % 2
            n_proj += 1
            pe.wait(m_ln[tt], *proj_free[bank])
            for k in range(KT):
                m = pe.do(lambda e, k=k: e.transpose(p_proj[:, bank, k * P:(k + 1) * P],
                                                     xn[:, j, k * P:(k + 1) * P], ident[:]),
                          s_xturn if k == KT - 1 else None)
            m_xturn[tt] = m
            src = p_proj[:, bank, :].rearrange("p (k t) -> p k t", k=KT)
            act.wait(m)
            if tt >= TPQ:
                act.wait(last_proj[tt // TPQ - 1])
            a = act.do(lambda e: e.activation(xt[:, 0, :, j * P:(j + 1) * P], src, ACT.Copy), s_xhi)
            dve.wait(a)
            d = dve.do(lambda e: e.tensor_tensor(xt[:, 1, :, j * P:(j + 1) * P], src,
                                                 xt[:, 0, :, j * P:(j + 1) * P].bitcast(F32), ALU.subtract), s_xlo)
            proj_free[bank] = [a, d]
            m_xparts[tt] = [a, d]

        last_proj = {}
        rt = {}

        def router_products(q):
            nonlocal misc_free
            pe.wait(m_wrp, *[m for t in range(TPQ) for m in m_xparts[q * TPQ + t]], *misc_free)
            terms = [(k, a) for k in range(KT) for a in (0, 1)]
            for n, (k, a) in enumerate(terms):
                m = pe.do(lambda e, n=n, k=k, a=a: e.matmul(
                    p_misc[0:2 * NX, 0:QT], wr_parts[:, k].rearrange("p a n -> p (a n)"), xt[:, a, k, :],
                    start=n == 0, stop=n == len(terms) - 1), s_pm if n == len(terms) - 1 else None)
            last_proj[q] = m
            act.wait(m)
            a = act.do(lambda e: e.activation(logitT[:], p_misc[0:2 * NX, 0:QT], ACT.Copy), s_ma)
            misc_free = [a]
            rt["T"] = a

        def rstep(emit, *marks):
            dve.wait(*marks)
            return dve.do(emit, s_rt)

        def route_turn(q):
            nonlocal misc_free
            pe.wait(rt["T"], *misc_free)
            for t in range(TPQ):
                m = pe.do(lambda e, t=t: e.transpose(p_misc[:, t * 2 * NX:(t + 1) * 2 * NX],
                                                     logitT[:, t * P:(t + 1) * P], ident[0:2 * NX, 0:2 * NX]), s_pm)
            both = p_misc[:, 0:TPQ * 2 * NX].rearrange("p (t a n) -> p t a n", t=TPQ, a=2)
            c = rstep(lambda e: e.tensor_copy(logit_lo[:], both[:, :, 1, :]), m)
            c = rstep(lambda e: e.tensor_tensor(logit[:], both[:, :, 0, :], logit_lo[:], ALU.add), c,
                      *rt.get("exp", []))
            misc_free = [c]
            rt["logit"] = c

        def choose(q):
            for t in range(TPQ):
                c = rstep(lambda e, t=t: e.max(top[:, t], logit[:, t, :]), rt["logit"])
            n = rstep(lambda e: e.tensor_scalar(ntop[:], top[:, :, 0], -1.0, None, ALU.mult), c, *rt.get("exp", []))
            for t in range(TPQ):
                c = rstep(lambda e, t=t: e.max_index(top_i[:, t], top[:, t], logit[:, t, :]))
            act.wait(n)
            if q:
                act.wait(rt["gate"])
            for t in range(TPQ):
                a = act.do(lambda e, t=t: e.activation(expl[:, t], logit[:, t, :], ACT.Exp, bias=ntop[:, t:t + 1],
                                                       accum_out=expsum[:, t:t + 1]), s_ma)
            rt["exp"] = [a]
            c = rstep(lambda e: e.tensor_copy(top_f[:], top_i[:, :, 0]), c)
            for t in range(TPQ):
                rt["onehot"] = rstep(lambda e, t=t: e.tensor_scalar(onehot[:, t, :], ex_iota[:], top_f[:, t:t + 1], None,
                                                                    ALU.is_equal), c, c_const, *rt.get("counted", []))

        def place(q):
            nonlocal misc_free
            new = q % 2
            pe.wait(rt["onehot"], *misc_free)
            if q:
                pe.wait(rt["seen"])
            for t in range(TPQ):
                cols = slice(t * NX, (t + 1) * NX)
                terms = ([(ones_bf, seen[:, 1 - new, :])] if q else []) + \
                    [(ones_bf, onehot[:, u, :]) for u in range(t)] + [(tri, onehot[:, t, :])]
                for i, (w_, v_) in enumerate(terms):
                    m = pe.do(lambda e, i=i, w_=w_, v_=v_, cols=cols, n=len(terms): e.matmul(
                        p_misc[:, cols], w_[:], v_, start=i == 0, stop=i == n - 1), s_pm)
            rt["counted"] = [m]
            if q:
                c = rstep(lambda e: e.tensor_tensor(seen[:, new, :], seen[:, 1 - new, :], onehot[:, 0, :], ALU.add))
            else:
                c = rstep(lambda e: e.tensor_copy(seen[:, new, :], onehot[:, 0, :]), rt["onehot"])
            for t in range(1, TPQ):
                c = rstep(lambda e, t=t: e.tensor_tensor(seen[:, new, :], seen[:, new, :], onehot[:, t, :], ALU.add), c)
            rt["seen"] = c
            for t in range(TPQ):
                c = rstep(lambda e, t=t: e.tensor_tensor_reduce(
                    pos_junk[:, t], onehot[:, t, :], p_misc[:, t * NX:(t + 1) * NX], 1.0, 0.0, ALU.mult, ALU.add,
                    pos[:, t:t + 1]), m)
            misc_free = [c]
            tiles = slice(q * TPQ, (q + 1) * TPQ)
            rstep(lambda e: e.tensor_scalar(rej[:], pos[:], float(CAP), FAR, ALU.is_gt, ALU.mult), c)
            c = rstep(lambda e: e.scalar_tensor_tensor(out=slot_f[:], in0=top_f[:], scalar=float(CAP),
                                                       in1=pos[:], op0=ALU.mult, op1=ALU.add))
            c = rstep(lambda e: e.scalar_tensor_tensor(out=slot_of[:, tiles], in0=slot_f[:], scalar=-1.0,
                                                       in1=rej[:], op0=ALU.add, op1=ALU.add), c)
            rt["gate"] = rstep(lambda e: e.reciprocal(id_gate[:, tiles, 1], expsum[:]), *rt["exp"])
            pool.wait(c, rt["gate"], m_tab)
            for tt in range(q * TPQ, (q + 1) * TPQ):
                pool.do(lambda e, tt=tt: e.indirect_dma_start(
                    out=slot_table[:, :], out_offset=bass.IndirectOffsetOnAxis(ap=slot_of[:, tt:tt + 1], axis=0),
                    in_=id_gate[:, tt, :], in_offset=None, bounds_check=SLOTS - 1, oob_is_err=False), s_scatter, 16)

        m_q, m_k = {}, {}

        def project(q, n, f):
            nonlocal n_proj
            which = n
            r = n_proj % 2
            n_proj += 1
            pe.wait(*m_weights, *[m for t in range(TPQ) for m in m_xparts[q * TPQ + t]], *proj_free[r])
            terms = [(k, a, b) for k in range(KT) for a, b in ((0, 0), (0, 1), (1, 0))]
            for i, (k, a, b) in enumerate(terms):
                m = pe.do(lambda e, i=i, k=k, a=a, b=b: e.matmul(
                    p_proj[:, r, 0:QT], wt[:, which, a, k, f * P:(f + 1) * P], xt[:, b, k, :],
                    start=i == 0, stop=i == len(terms) - 1), s_proj if i == len(terms) - 1 else None)
            last_proj[q] = m
            act.wait(m, m_w[which], *stage_free[f // 2])
            b = bias[:, which, f:f + 1]
            hi = stage[:, 0, f, :]
            a = act.do(lambda e: e.activation(hi, p_proj[:, r, 0:QT], ACT.Identity, bias=b), s_phi)
            dve.wait(a)
            d = dve.do(lambda e: e.scalar_tensor_tensor(out=stage[:, 1, f, :], in0=p_proj[:, r, 0:QT], scalar=b,
                                                        in1=hi.bitcast(F32), op0=ALU.add, op1=ALU.subtract), s_plo)
            proj_free[r] = [d]
            if f % 2 == 1:
                sp.wait(d)
                move(q, which, f // 2)

        def project_v(q, t):
            nonlocal n_proj
            r = n_proj % 2
            n_proj += 1
            pe.wait(*m_weights, *[m for u in range(TPQ) for m in m_xparts[q * TPQ + u]], *proj_free[r])
            terms = [(k, a, b) for k in range(KT) for a, b in ((0, 0), (0, 1), (1, 0))]
            for i, (k, a, b) in enumerate(terms):
                m = pe.do(lambda e, i=i, k=k, a=a, b=b: e.matmul(
                    p_proj[:, r, :], xt[:, a, k, t * P:(t + 1) * P], wt[:, 2, b, k, :],
                    start=i == 0, stop=i == len(terms) - 1), s_proj if i == len(terms) - 1 else None)
            last_proj[q] = m
            dve.wait(m, m_bv, *stage_v_free)
            d = dve.do(lambda e: e.tensor_tensor(stage_v[:, t, :], p_proj[:, r, :], bias_v[:], ALU.add), s_plo)
            proj_free[r] = [d]
            if t < TPQ - 1:
                return
            sp.wait(d)
            m = sp.do(lambda e: e.dma_start(v_rows[q * QT:(q + 1) * QT, :].rearrange("(t p) e -> p t e", p=P),
                                            stage_v[:]), s_vst, 16)
            stage_v_free[:] = [m]
            m_vstored[q] = m

        m_vstored = {}

        def fetch_v(q):
            sp.wait(m_vstored[q])
            if q >= 2:
                sp.wait(m_pv[(q - 2) * NT + NT - 1], m_vread[q - 2])
            heads = v_rows[q * QT:(q + 1) * QT, :].rearrange("(g t) (c d) -> g (t c) d", g=QH, d=D)
            for g in range(QH):
                m = sp.do(lambda e, g=g: e.dma_start(vn[:, q % 2, :, g * D:(g + 1) * D],
                                                     heads[g].rearrange("(n p) d -> p n d", p=P)), s_v[q % 2], 16)
            m_vn[q] = m

        stage_free, stage_v_free, q_land_free = [[], []], [], []

        def landing(q, which):
            return (q_land, s_q, m_q, 0, 1, 2) if which == 0 else (ks[q % 2], s_k[q % 2], m_k, 0, 2, 1)

        def move(q, which, half):
            dst, landed, marks, hi_row, lo_row, _ = landing(q, which)
            if which == 0:
                sp.wait(*q_land_free)
            elif q >= 2:
                sp.wait(m_scored[(q - 2) * NT + NT - 1])
            for part, row in enumerate((hi_row, lo_row)):
                for c4 in range(4):
                    m = sp.do(lambda e, row=row, part=part, c4=c4: e.dma_start(
                        dst[row * D:(row + 1) * D, 8 * half + c4:8 * half + c4 + 5:4, :].bitcast(F32),
                        stage[c4 * D:(c4 + 1) * D, part, 2 * half:2 * half + 2, :].bitcast(F32)), landed[half], 16)
            stage_free[half] = [m]
            marks.setdefault(q, []).append(m)

        def double(q, which):
            dst, landed, marks, hi_row, _, again = landing(q, which)
            sp.wait(*marks[q])
            marks[q].append(sp.do(lambda e: e.dma_start(dst[again * D:(again + 1) * D, :, :].bitcast(F32),
                                                   dst[hi_row * D:(hi_row + 1) * D, :, :].bitcast(F32)),
                                  landed[2], 16))

        m_qcopy, m_vcopy, m_scored = {}, {}, {}

        def copy_q(q, j):
            pool.wait(*m_q[q])
            if q:
                pool.wait(m_scored[(q - 1) * NT + 2 * j + 1])
            w = 2 * TT
            src = q_land[:].bitcast(F32).rearrange("p c (g t) -> p g t c", g=QH)
            dst = qn[:].rearrange("p (g t) c -> p g t c", g=QH)
            m_qcopy[q, j] = pool.do(lambda e: e.tensor_copy(dst[:, :, j * w:(j + 1) * w, :],
                                                            src[:, :, j * w:(j + 1) * w, :]), s_copy)
            if j == 3:
                q_land_free[:] = [m_qcopy[q, j]]

        m_vn, m_far, m_vread = {}, {}, {}

        def far_sums(q):
            nonlocal misc_free
            par = q % 2
            pe.wait(m_vn[q], *misc_free)
            for t in range(NT):
                m = pe.do(lambda e, t=t: e.matmul(p_misc[:, 2 * t:2 * t + 2], vn[:, par, t, :], ones2[:], start=True,
                                                  stop=True), s_pm if t == NT - 1 else None)
            m_vread[q] = m
            src = p_misc[:, 0:2 * NT].rearrange("p (t two) -> p t two", two=2)[:, :, 0]
            dve.wait(m)
            c = dve.do(lambda e: e.tensor_copy(vsum[:, 0, :], src), s_md)
            dve.wait(c)
            c = dve.do(lambda e: e.tensor_tensor(vsum[:, 1, :], src, vsum[:, 0, :].bitcast(F32), ALU.subtract), s_md)
            misc_free = [c]
            m_vsum[q] = c

        m_vsum = {}

        def far_sums_turn(q):
            nonlocal misc_free
            pe.wait(m_vsum[q], *misc_free)
            m = pe.do(lambda e: e.transpose(p_misc[0:2 * NT, 0:P],
                                            vsum[:].rearrange("p a t -> p (a t)").bitcast(F32), ident[:]), s_pm)
            act.wait(m)
            a = act.do(lambda e: e.activation(far_rows[:, q % 2, :], p_misc[0:2 * NT, 0:P], ACT.Copy), s_ma)
            misc_free = [a]
            m_far[q] = a

        score_free = [[], []]
        prob_free = [[] for _ in range(SR)]
        prob_free[0] = [m_tab]
        m_exp, m_negm = {}, {}
        m_eout = {}
        m_row_free = {}
        n_score = 0

        def window(T):
            first = max(T - 1, 0)
            return first, min(T + 2, NT) - first

        def scores(s, g):
            nonlocal n_score
            q, T = divmod(s, NT)
            par = q % 2
            first, nj = window(T)
            w = nj * TT
            m_lo = 0 if T else TT
            r = n_score % 2
            slot = n_score % SR
            row = g * HT
            pe.wait(m_qcopy[q, T // 2], *m_k[q], *score_free[r])
            m = pe.do(lambda e: e.matmul(
                p_score[:, r, 0:CH * w],
                qn[:, row + T * TT:row + (T + 1) * TT, :].rearrange("p t c -> p (t c)"),
                ks[par][:, :, row + first * TT:row + first * TT + w], start=True, stop=True), s_score)
            m_scored[s] = m
            dve.wait(m, c_const, *prob_free[slot])
            if g == 0 and q >= 2:
                dve.wait(m_row_free[q - 2])
            d = dve.do(lambda e: e.tensor_tensor_reduce(
                prob[:, slot, 0:CH * w].rearrange("p (t c) -> p c t", c=CH),
                p_score[:, r, 0:CH * w].rearrange("p (c t) -> p c t", c=CH),
                mask[:, :, m_lo:m_lo + w], 1.0, 0.0, ALU.mult, ALU.max, row_max[:, par, T, g:g + 1]), s_masked)
            score_free[r] = [d]
            slots_of.setdefault(s, []).append(slot)
            n_score += 1

        slots_of = {}

        def weights(s, pair):
            q, T = divmod(s, NT)
            par = q % 2
            w = window(T)[1] * TT
            two = slice(2 * pair, 2 * pair + 2)
            dve.wait((s_masked, s_masked.value))
            c = dve.do(lambda e: e.tensor_scalar(neg_max[:, par, T, two], row_max[:, par, T, two], -SCALE, None,
                                                 ALU.mult), s_negm)

            def exps():
                act.wait(c)
                for g in (2 * pair, 2 * pair + 1):
                    slot = slots_of[s][g]
                    a = act.do(lambda e, g=g, slot=slot: e.activation(
                        prob[:, slot, 0:CH * w], prob[:, slot, 0:CH * w], ACT.Exp, bias=neg_max[:, par, T, g:g + 1],
                        scale=SCALE, accum_out=row_sum[:, par, T, g:g + 1]), s_exp)
                if pair == 1:
                    m_exp[s] = (a, slots_of[s])
                    m_eout[s] = act.do(lambda e: e.activation(e_out[:, par, T, :], neg_max[:, par, T, :], ACT.Exp),
                                       s_exp)
            return exps

        turn_free = [[], []]
        n_turn = 0
        m_probT, m_pv, turn_step, place_of = {}, {}, {}, {}

        def turn_probs(s, jj):
            nonlocal n_turn
            q, T = divmod(s, NT)
            first, nj = window(T)
            if jj >= nj:
                return
            r = n_turn % 2
            mark, slots = m_exp[s]
            pe.wait(mark, *turn_free[r])
            for g, slot in enumerate(slots):
                m = pe.do(lambda e, g=g, slot=slot: e.transpose(
                    p_turn[:, r, g * P:(g + 1) * P], prob[:, slot, jj * P:(jj + 1) * P], ident[:]),
                    s_turn if g == QH - 1 else None)
            if jj == nj - 1:
                for slot in slots:
                    prob_free[slot] = [m]
            eng, cnt = (dve, s_turnedD) if jj == 1 else (act, s_turnedA)
            eng.wait(m)
            if n_turn >= PR:
                eng.wait(m_pv[turn_step[n_turn - PR]])
            turn_step[n_turn] = s
            dst = probT[:, n_turn % PR, :]
            place_of[s, jj] = n_turn % PR
            if eng is act:
                a = act.do(lambda e: e.activation(dst, p_turn[:, r, :], ACT.Copy), cnt)
            else:
                a = dve.do(lambda e: e.tensor_copy(dst, p_turn[:, r, :]), cnt)
            turn_free[r] = [a]
            m_probT.setdefault(s, []).append(a)
            n_turn += 1

        att_free = []

        def weigh(s):
            q, T = divmod(s, NT)
            par = q % 2
            first, nj = window(T)
            pe.wait(m_vn[q], *m_probT[s], *(att_free if T % 4 == 0 else []))
            col = (T % 4) * P
            for jj in range(nj):
                for g in range(QH):
                    m = pe.do(lambda e, jj=jj, g=g: e.matmul(
                        p_att[g * D:(g + 1) * D, col:col + P], vn[:, par, first + jj, g * D:(g + 1) * D],
                        probT[:, place_of[s, jj], g * P:(g + 1) * P], start=jj == 0, stop=jj == nj - 1,
                        skip_group_check=True), s_pv if jj == nj - 1 and g == QH - 1 else None)
            m_pv[s] = m

        m_addend = {}

        def far_part(s):
            nonlocal misc_free, att_free
            q, T = divmod(s, NT)
            half, par = T // 4, q % 2
            t0 = half * 4
            act.wait(m_pv[s])
            if m_addend:
                act.wait(m_addend["attT"])
            a = act.do(lambda e: e.activation(attT[:], p_att[:], ACT.Copy), s_att)
            att_free = [a]
            pe.wait(m_far[q], c_pick, *misc_free)
            for t in range(4):
                m = pe.do(lambda e, t=t: e.matmul(p_misc[:, t * P:(t + 1) * P], far_pick_r[:, t0 + t:t0 + t + 1].broadcast_to([2 * NT, P]),
                                                  far_rows[:, par, :], start=True, stop=True),
                          s_pm if t == 3 else None)
            m_far_sum[s] = (a, m)

        m_far_sum = {}

        def far_weigh(s):
            nonlocal misc_free
            q, T = divmod(s, NT)
            half, par = T // 4, q % 2
            t0 = half * 4
            a, m = m_far_sum[s]
            eo = e_out[:, par, t0:t0 + 4, :].rearrange("p t g -> p (t g)")
            tg = 4 * QH

            def wide(v):
                return v.unsqueeze(2).broadcast_to([P, tg, D])

            def cols(v):
                return v.rearrange("p (n d) -> p n d", d=D)

            dve.wait(m, m_eout[s], *m_addend.get("far_e", []))
            d = dve.do(lambda e: e.tensor_tensor(cols(far_e[:]), cols(p_misc[:]), wide(eo), ALU.mult), s_post)
            misc_free = [d]
            den_v = den[:, par, t0:t0 + 4, :].rearrange("p t g -> p (t g)")
            rden_v = rden[:, par, t0:t0 + 4, :].rearrange("p t g -> p (t g)")
            c = dve.do(lambda e: e.tensor_tensor(den_v, n_out[:, t0:t0 + 4, :].rearrange("p t g -> p (t g)"), eo,
                                                 ALU.mult), s_post)
            dve.wait(c)
            c = dve.do(lambda e: e.tensor_tensor(den_v, den_v, row_sum[:, par, t0:t0 + 4, :].rearrange(
                "p t g -> p (t g)"), ALU.add), s_post)
            dve.wait(c)
            c = dve.do(lambda e: e.reciprocal(rden_v, den_v), s_post)
            m_far_e[s] = (a, d, c)

        m_far_e = {}

        def finish(s):
            nonlocal misc_free
            q, T = divmod(s, NT)
            half, par = T // 4, q % 2
            t0 = half * 4
            a, d, c = m_far_e[s]

            def cols(v):
                return v.rearrange("p (n d) -> p n d", d=D)

            pe.wait(a, *misc_free)
            for t in range(4):
                m = pe.do(lambda e, t=t: e.transpose(p_misc[:, t * P:(t + 1) * P], attT[:, t * P:(t + 1) * P],
                                                     ident[:]), s_pm if t == 3 else None)
            m_addend["attT"] = m
            dve.wait(m, d)
            d = dve.do(lambda e: e.tensor_tensor(far_e[:], p_misc[:], far_e[:], ALU.add), s_post)
            misc_free = [d]
            b, qd = divmod(q, QB)
            pool.wait(d, c)
            if qd == 0:
                for t in range(4):
                    pool.wait(*ao_free[t0 + t])
            for_t = ao[:, t0:t0 + 4, qd * P:(qd + 1) * P].rearrange("p t (g d) -> p t g d", d=D)
            tiles = far_e[:].rearrange("p (t g d) -> p t g d", t=4, g=QH)
            rd = rden[:, par, t0:t0 + 4, :]
            for t in range(4):
                d = pool.do(lambda e, t=t: e.tensor_tensor(
                    for_t[:, t], tiles[:, t], rd[:, t].unsqueeze(2).broadcast_to([P, QH, D]), ALU.mult), s_norm)
            m_addend["far_e"] = [d]
            if half == 1:
                m_row_free[q] = d
            if qd == QB - 1:
                late_jobs.extend((b, t0 + t, d) for t in range(4))

        late_jobs, late_stage = [], []
        late_place = [late[:], stage_v[:, 0, :], stage_v[:, 1, :]]
        n_late = 0

        def late_load():
            nonlocal n_late
            if not late_jobs:
                return
            b, t, done = late_jobs.pop(0)
            tt = b * NT + t
            r = n_late % LR if b == B - 1 else 0
            n_late += 1
            sp.wait(m_sum[tt], *late_free[r], *(stage_v_free if r else []))
            m = sp.do(lambda e: e.dma_start(late_place[r], sum_rows[tt * P:(tt + 1) * P, :]), s_late[r], 16)
            late_stage.append((t, tt, r, m, done))

        def late_add(ahead):
            if len(late_stage) < (ahead if late_jobs else 1):
                return
            t, tt, r, m, done = late_stage.pop(0)
            pool.wait(m, done)
            m = pool.do(lambda e: e.tensor_tensor(ao[:, t, :], ao[:, t, :], late_place[r], ALU.add), s_resdone)
            late_free[r] = [m]
            return t, tt, m

        def late_store(job):
            if not job:
                return
            t, tt, m = job
            sp.wait(m)
            m1 = sp.do(lambda e: e.dma_start(out_rows[tt * P:(tt + 1) * P, :], ao[:, t, :]), s_store[t], 16)
            m2 = sp.do(lambda e: e.dma_start(base_rows[tt * P:(tt + 1) * P, :], ao[:, t, :]), s_base[t], 16)
            ao_free[t] = [m1, m2]

        for tt in range(TPQ):
            load_x(tt)
        norm_stats(0)
        norm_stats(1)
        norm_scale(0)
        for tt in range(TPQ):
            layer_norm(tt)
            load_x(tt + TPQ)
            turn_x(tt)
        for f in range(KT):
            project(0, 0, f)
        for f in range(KT):
            project(0, 1, f)
        double(0, 0)
        double(0, 1)
        for t in range(TPQ):
            project_v(0, t)
        fetch_v(0)
        for j in range(4):
            copy_q(0, j)
        router_products(0)
        norm_stats(2)
        norm_stats(3)
        norm_scale(1)
        for tt in range(TPQ, 2 * TPQ):
            layer_norm(tt)
            load_x(tt + TPQ)
        route_turn(0)
        choose(0)
        place(0)
        for tt in range(TPQ, 2 * TPQ):
            turn_x(tt)
        NS = NQ * NT
        CHUNKS = [[("q", 0), ("q", 1)], [("q", 2), ("q", 3)], [("k", 0), ("k", 1)], [("k", 2)], [("k", 3)],
                  [("v", 0)], [("v", 1)], []]

        def chunk(q, T, n):
            if q + 1 < NQ and n < len(CHUNKS[T]):
                what, part = CHUNKS[T][n]
                if what == "v":
                    project_v(q + 1, part)
                else:
                    project(q + 1, "qk".index(what), part)

        def misc_first(s):
            q, T = divmod(s, NT)
            here, ahead = q < NQ, q + 1 < NQ
            if T == 0 and ahead:
                router_products(q + 1)
            if T == 1 and ahead:
                route_turn(q + 1)
            if T == 2 and here:
                far_sums(q)
            if T == 3 and here:
                far_sums_turn(q)

        def misc_second(s):
            q, T = divmod(s, NT)
            here, ahead = q < NQ, q + 1 < NQ
            if T == 0 and 0 < q <= NQ or T == 4 and here:
                far_part(s - 1)
            if T == 1 and 0 < q <= NQ or T == 5 and here:
                finish(s - 2)
            if T == 3 and ahead:
                place(q + 1)

        for pair in (0, 1):
            scores(0, 2 * pair)
            scores(0, 2 * pair + 1)
            weights(0, pair)()
        def step(s):
            q, T = divmod(s, NT)
            ahead, more = q + 1 < NQ, s + 1 < NS
            if ahead and T == 2:
                double(q + 1, 0)
            if ahead and T == 5:
                double(q + 1, 1)
            if ahead and T == 7:
                fetch_v(q + 1)
            late_sum = late_add(LR if s >= NS else 1)
            late_load()
            if more:
                scores(s + 1, 0)
            chunk(q, T, 0)
            if T == 7 and q + 2 < NQ:
                turn_x((q + 2) * TPQ)
            if T == 1 and 0 < q <= NQ or T == 5 and q < NQ:
                far_weigh(s - 2)
            if s < NS:
                turn_probs(s, 0)
            if more:
                scores(s + 1, 1)
                exps = weights(s + 1, 0)
            if T == 7 and q + 2 < NQ:
                turn_x((q + 2) * TPQ + 1)
            misc_first(s)
            if T == 2 and ahead:
                choose(q + 1)
            if more:
                exps()
            if s < NS:
                turn_probs(s, 1)
            if more:
                scores(s + 1, 2)
            if 1 <= s <= NS:
                weigh(s - 1)
            if more:
                scores(s + 1, 3)
                weights(s + 1, 1)()
            chunk(q, T, 1)
            if s < NS:
                turn_probs(s, 2)
            misc_second(s)
            if q + 2 < NQ:
                if T in (0, 1):
                    norm_stats((q + 2) * TPQ + T)
                if T == 2:
                    norm_scale(q + 2)
                if T in (3, 4):
                    layer_norm((q + 2) * TPQ + T - 3)
            if ahead and T in (4, 5, 6, 7):
                copy_q(q + 1, T - 4)
            if T in (5, 6) and q + 3 < NQ:
                load_x((q + 3) * TPQ + T - 5)
            late_store(late_sum)

        tab_rows = q_land[0:NX, :, :].bitcast(F32).rearrange("n c t -> n (c t)")[:, 0:2 * CAP]

        def read_table():
            sp.wait((s_scatter, s_scatter.value))
            sp.wait(*q_land_free)
            return sp.do(lambda e: e.dma_start(tab_rows, slot_table.rearrange("(n c) two -> n (c two)", n=NX)),
                         s_tabin, 16)

        def turn_table(m_tabin):
            nonlocal misc_free
            pe.wait(m_tabin, *misc_free)
            rows = tab_rows.rearrange("n (c two) -> n c two", two=2)
            for r in range(NR):
                for v in range(2):
                    m = pe.do(lambda e, r=r, v=v: e.transpose(
                        p_misc[0:wide_of[r], (2 * r + v) * NX:(2 * r + v + 1) * NX],
                        rows[:, r * P:r * P + wide_of[r], v], ident[0:NX, 0:NX]), s_pm)
            dve.wait(m)
            for r in range(NR):
                w = wide_of[r]
                dve.do(lambda e, r=r, w=w: e.tensor_copy(token_of[0:w, r, :],
                                                         p_misc[0:w, 2 * r * NX:(2 * r + 1) * NX]), s_dt)
                c = dve.do(lambda e, r=r, w=w: e.tensor_copy(gate_of[0:w, r, :],
                                                             p_misc[0:w, (2 * r + 1) * NX:(2 * r + 2) * NX]), s_dt)
            misc_free = [c]
            return c

        for s in range(NS - 1):
            step(s)
            if s == NS - NT:
                m_tabin = read_table()
            if s == NS - 3:
                c_tab = turn_table(m_tabin)

        c1.close()

        RW = 4
        RS = 4
        wraw = sb("wraw", [P, RW, KT, FF])
        xg = sb("xg", [P, 2, NR, E])
        yb = sb("yb", [P, 2, NR, E])
        xe = sb("xe", [P, 2, 2, KT, CAP], F32R)
        wsplit = sb("wsplit", [P, RS, 2, KT, FF], F32R)
        sg = sb("sg", [P, 2, CAP])
        hid = sb("hid", [P, 2, CAP])
        hparts = sb("hparts", [P, 2, KT, CAP], F32R)

        s_clear = sem("s_clear")
        s_wr = [sem(f"s_wr{i}") for i in range(RW)]
        s_whi = sem("s_whi")
        s_wloD = sem("s_wlo_dve")
        s_wloP = sem("s_wlo_pool")
        s_xg = [sem(f"s_xg{i}") for i in range(2)]
        s_yb = [sem(f"s_yb{i}") for i in range(2)]
        s_ys = [sem(f"s_ys{i}") for i in range(2)]
        s_xeP = sem("s_xe_pe")
        s_xeA = sem("s_xe_act")
        s_xeD = sem("s_xe_dve")
        s_gu = sem("s_gu")
        s_sg = sem("s_sg")
        s_hid = sem("s_hid")
        s_hhi = sem("s_hhi")
        s_hlo = sem("s_hlo")
        s_down = sem("s_down")
        s_y = sem("s_y")


        m_wr2, m_wsplit, m_used = {}, {}, {}

        def load_w(i):
            x_, which = divmod(i, 3)
            src = (w_gate, w_up, w_down)[which]
            if i >= RW:
                sp.wait(*m_wsplit[i - RW])
            m_wr2[i] = sp.do(lambda e: e.dma_start(wraw[:, i % RW], src[x_].rearrange("(k p) f -> p k f", p=P)),
                             s_wr[i % RW], 16)

        def split_w(i):
            r, t = i % RW, i % RS
            act.wait(m_wr2[i])
            if i >= RS:
                act.wait(m_used[i - RS])
            a = act.do(lambda e: e.activation(wsplit[:, t, 0], wraw[:, r], ACT.Copy), s_whi)
            eng, cnt = (pool, s_wloP) if i % 3 == 2 else (dve, s_wloD)
            eng.wait(a)
            d = eng.do(lambda e: e.tensor_tensor(wsplit[:, t, 1], wraw[:, r], wsplit[:, t, 0].bitcast(F32),
                                                 ALU.subtract), cnt)
            m_wsplit[i] = [a, d]

        m_xg, m_yb, m_xeturn, m_ys, m_xe = {}, {}, {}, {}, {}

        def gather(x_, n):
            p2 = x_ % 2
            dst, src, cnt, marks = ((xg, xn_rows, s_xg, m_xg), (yb, base_rows, s_yb, m_yb))[n]
            pool.wait(c_tab, c_clear_y if n else c_clear_x)
            if x_ >= 2:
                pool.wait((m_xeturn, m_ys)[n][x_ - 2])
            for r in range(NR):
                w = wide_of[r]
                marks[x_] = pool.do(lambda e, r=r, w=w: e.indirect_dma_start(
                    out=dst[0:w, p2, r, :], out_offset=None, in_=src[:, :],
                    in_offset=bass.IndirectOffsetOnAxis(ap=token_of[0:w, r, x_:x_ + 1], axis=0),
                    bounds_check=TOK - 1, oob_is_err=False), cnt[p2], 16)

        def turn_xe(x_, r):
            nonlocal misc_free
            p2 = x_ % 2
            pe.wait(m_xg[x_])
            if True:
                w = wide_of[r]
                bank = p_misc
                pe.wait(*misc_free)
                for k in range(KT):
                    m = pe.do(lambda e, r=r, w=w, k=k, bank=bank: e.transpose(
                        bank[:, k * w:(k + 1) * w], xg[0:w, p2, r, k * P:(k + 1) * P], ident[0:w, 0:w]),
                        s_xeP if k == KT - 1 else None)
                src = bank[:, 0:KT * w].rearrange("p (k t) -> p k t", k=KT)
                act.wait(m)
                if x_ >= 2:
                    act.wait(m_gu_last[x_ - 2])
                hi = xe[:, p2, 0, :, r * P:r * P + w]
                lo = xe[:, p2, 1, :, r * P:r * P + w]
                a = act.do(lambda e, hi=hi, src=src: e.activation(hi, src, ACT.Copy), s_xeA)
                dve.wait(a)
                d = dve.do(lambda e, hi=hi, lo=lo, src=src: e.tensor_tensor(lo, src, hi.bitcast(F32), ALU.subtract),
                           s_xeD)
                misc_free = [a, d]
                m_xe.setdefault(x_, []).extend((a, d))
            m_xeturn[x_] = m

        m_gu_last, m_h = {}, {}
        gu_free = [[], []]
        h_free = []
        PARTS = ((0, 0), (0, 1), (1, 0))

        def gate_up(x_, f):
            n = x_ * KT + f
            r, p2 = n % 2, x_ % 2
            for which, bank in ((0, p_score), (1, p_turn)):
                i = 3 * x_ + which
                pe.wait(*m_wsplit[i], *m_xe[x_], *gu_free[r])
                terms = [(k, a, b) for k in range(KT) for a, b in PARTS]
                for j, (k, a, b) in enumerate(terms):
                    m = pe.do(lambda e, j=j, k=k, a=a, b=b, bank=bank, i=i: e.matmul(
                        bank[:, r, 0:CAP], wsplit[:, i % RS, a, k, f * P:(f + 1) * P], xe[:, p2, b, k, :],
                        start=j == 0, stop=j == len(terms) - 1), s_gu if j == len(terms) - 1 else None)
                m_used[i] = m
                if which == 0:
                    m_g = m
            m_gu_last[x_] = m
            g_, u_ = p_score[:, r, 0:CAP], p_turn[:, r, 0:CAP]
            act.wait(m_g)
            if n >= 2:
                act.wait(sg_marks[n - 2])
            a = act.do(lambda e: e.activation(sg[:, r], g_, ACT.Silu), s_sg)
            dve.wait(a, m)
            if n >= 2:
                dve.wait(m_h[n - 2][0])
            c = dve.do(lambda e: e.tensor_tensor(hid[:, r], sg[:, r], u_, ALU.mult), s_hid)
            sg_marks[n] = c
            gu_free[r] = [c]
            act.wait(c, *h_free)
            a = act.do(lambda e: e.activation(hparts[:, 0, f, :], hid[:, r], ACT.Copy), s_hhi)
            dve.wait(a)
            d = dve.do(lambda e: e.tensor_tensor(hparts[:, 1, f, :], hid[:, r], hparts[:, 0, f, :].bitcast(F32),
                                                 ALU.subtract), s_hlo)
            m_h[n] = [a, d]

        sg_marks = {}
        ybank = [p_proj[:, 0, :], p_proj[:, 1, :], p_att[:]]
        n_y = 0

        def down(x_):
            nonlocal n_y, h_free
            p2, i = x_ % 2, 3 * x_ + 2
            last = []
            for r in range(NR):
                w = wide_of[r]
                b2 = n_y % 3
                pe.wait(*m_wsplit[i], *y_free[b2])
                terms = [(f, a, b) for f in range(KT) for a, b in PARTS]
                for j, (f, a, b) in enumerate(terms):
                    pe.wait(*m_h[x_ * KT + f])
                    m = pe.do(lambda e, j=j, f=f, a=a, b=b, w=w, b2=b2, r=r: e.matmul(
                        ybank[b2][0:w, :], hparts[:, a, f, r * P:r * P + w], wsplit[:, i % RS, b, f, :],
                        start=j == 0, stop=j == len(terms) - 1), s_down if j == len(terms) - 1 else None)
                dve.wait(m, m_yb[x_])
                d = dve.do(lambda e, w=w, b2=b2, r=r: e.scalar_tensor_tensor(
                    out=yb[0:w, p2, r, :], in0=ybank[b2][0:w, :], scalar=gate_of[0:w, r, x_:x_ + 1],
                    in1=yb[0:w, p2, r, :], op0=ALU.mult, op1=ALU.add), s_y)
                y_free[b2] = [d]
                last.append(d)
                n_y += 1
            m_used[i] = m
            h_free = [m]
            pend.append((x_, last))

        pend = []

        def scatter(x_, last):
            p2 = x_ % 2
            for r in range(NR):
                w = wide_of[r]
                pool.wait(last[r])
                m_ys[x_] = pool.do(lambda e, r=r, w=w: e.indirect_dma_start(
                    out=out_rows[:, :], out_offset=bass.IndirectOffsetOnAxis(ap=token_of[0:w, r, x_:x_ + 1], axis=0),
                    in_=yb[0:w, p2, r, :], in_offset=None, bounds_check=TOK - 1, oob_is_err=False), s_ys[p2], 16)

        sp.wait(last_proj[NQ - 1])
        for i in range(RW):
            load_w(i)
        dve.wait(last_proj[NQ - 1])
        c_clear_x = dve.do(lambda e: e.memset(xg[:], 0.0), s_clear)
        pool.wait(*[m_xnst[tt] for tt in range((NQ - 1) * TPQ, NQ * TPQ)])
        gather(0, 0)
        gather(1, 0)
        step(NS - 1)
        end1 = [(c, c.value) for c in (
            s_const, s_scatter, s_ln, s_newton, s_resadd, s_xturn, s_xhi, s_xlo, s_proj, s_phi, s_plo, s_score,
            s_masked, s_negm, s_exp, s_turn, s_turnedA, s_turnedD, s_pm, s_ma, s_md, s_rt, s_load, s_bv, s_vst, s_pw,
            s_aw, s_dw, s_tab, *s_sum, *s_xnst, *s_x, *s_q, *s_k[0], *s_k[1], *s_v, s_copy, *s_wraw) if c.value]
        for eng in (act, dve):
            eng.wait(*end1)
        gu_free = [score_free[0] + turn_free[0], score_free[1] + turn_free[1]]
        split_w(0)
        load_w(RW)
        turn_xe(0, 0)
        step(NS)
        split_w(1)
        load_w(RW + 1)
        step(NS + 1)
        turn_xe(0, 1)
        split_w(2)
        load_w(RW + 2)
        turn_xe(0, 2)
        c_clear_y = dve.do(lambda e: e.memset(yb[:], 0.0), s_clear)
        s = NS + 2
        while late_jobs or late_stage:
            step(s)
            s += 1
        y_free = [proj_free[0], proj_free[1], att_free]
        pool.wait(*[m for t in range(NT) for m in ao_free[t]])
        gather(0, 1)

        def next_w(x_, which):
            i = 3 * (x_ + 1) + which
            if i < 3 * NX:
                split_w(i)
                if i + RW < 3 * NX:
                    load_w(i + RW)

        for x_ in range(NX):
            if x_ + 2 < NX:
                gather(x_ + 2, 0)
            for f in range(KT):
                gate_up(x_, f)
                if f == 1 and x_ + 1 < NX:
                    gather(x_ + 1, 1)
                if f == 0:
                    next_w(x_, 0)
                elif x_ + 1 < NX:
                    turn_xe(x_ + 1, f - 1)
            next_w(x_, 1)
            next_w(x_, 2)
            down(x_)
            scatter(*pend.pop())

        sp.wait(*[(c, c.value) for c in s_ys])

        block = ctx.enter_context(nc.Block())

        @block.tensor
        def _(e):
            pe.play(e)

        @block.scalar
        def _(e):
            act.play(e)

        @block.vector
        def _(e):
            dve.play(e)

        @block.gpsimd
        def _(e):
            pool.play(e)

        @block.sync
        def _(e):
            sp.play(e)


_INS = ["L0_attn_x", "L0_attn_Wq", "L0_attn_bq", "L0_attn_Wk", "L0_attn_bk", "L0_attn_Wv", "L0_attn_bv",
        "L0_ffn_w_router", "L0_ffn_w_gate", "L0_ffn_w_up", "L0_ffn_w_down"]


def kernel(**inputs):
    import concourse.bacc as bacc
    from concourse.bass_utils import run_bass_kernel_spmd

    nc = bacc.Bacc("TRN2", target_bir_lowering=False, num_devices=1)
    arrays, args = {}, []
    for name in _INS:
        a = np.ascontiguousarray(inputs[name])
        arrays[f"in_{name}"] = a
        args.append(nc.dram_tensor(f"in_{name}", a.shape, mybir.dt.from_np(a.dtype), kind="ExternalInput").ap())
    shape = inputs["L0_attn_x"].shape
    out = nc.dram_tensor("out_x", shape, F32, kind="ExternalOutput").ap()
    build(nc, *args, out)
    r = run_bass_kernel_spmd(nc, [arrays], core_ids=[0])
    return r.results[0]["out_x"]
```

```python
from contextlib import ExitStack

import numpy as np
import concourse.bass as bass
from concourse import mybir

ALU = mybir.AluOpType
ACT = mybir.ActivationFunctionType
F32 = mybir.dt.float32
F32R = mybir.dt.float32r
BF16 = mybir.dt.bfloat16
U32 = mybir.dt.uint32
I32 = mybir.dt.int32
AX = mybir.AxisListType

P = 128


class Counter:

    def __init__(self, handle):
        self.handle = handle
        self.value = 0


class Queue:

    def __init__(self):
        self.steps = []
        self.waited = {}

    def wait(self, *marks):
        for counter, value in marks:
            if self.waited.get(counter, 0) < value:
                self.waited[counter] = value
                self.steps.append((counter.handle, value))

    def do(self, emit, counter=None, by=1):
        if counter is None:
            self.steps.append((emit,))
            return None
        counter.value += by
        self.steps.append((emit, counter.handle, by))
        return (counter, counter.value)

    def play(self, engine):
        for step in self.steps:
            if len(step) == 2:
                engine.wait_ge(step[0], step[1])
            elif len(step) == 1:
                step[0](engine)
            else:
                step[0](engine).then_inc(step[1], step[2])


def build(nc, x, Wq, bq, Wk, bk, Wv, bv, w_router, w_gate, w_up, w_down, out):
    B, S, E = x.shape
    H = 16
    D = E // H
    CH = E // D
    HT = S // CH
    BAND = 128
    TOK = B * S
    NX, _, FF = w_gate.shape
    CAP = -(-5 * TOK // (4 * NX))
    SLOTS = NX * CAP
    KT = E // P
    QH = 4
    QT = QH * HT
    NQ = TOK // QT
    QB = H // QH
    NT = S // P
    TT = P // CH
    TPQ = QT // P
    XR = 2
    PR = 6
    SR = 8
    LR = 1 + TPQ
    NR = -(-CAP // P)
    wide_of = [min(P, CAP - r * P) for r in range(NR)]
    SCALE = float(D) ** -0.5
    FAR = float(1 << 20)
    assert BAND == P and QT == 256 and TT == 8 and FF == E and E == 512

    Q = {n: Queue() for n in ("pe", "act", "dve", "pool", "sp")}
    pe, act, dve, pool, sp = (Q[n] for n in ("pe", "act", "dve", "pool", "sp"))

    x_rows = x.rearrange("b s e -> (b s) e")
    out_rows = out.rearrange("b s e -> (b s) e")
    xn_rows = nc.dram_tensor("xn_rows", [TOK, E], F32, kind="Internal").ap()
    sum_rows = nc.dram_tensor("sum_rows", [TOK, E], F32, kind="Internal").ap()
    base_rows = nc.dram_tensor("base_rows", [TOK, E], F32, kind="Internal").ap()
    v_rows = nc.dram_tensor("v_rows", [TOK, E], F32, kind="Internal").ap()
    slot_table = nc.dram_tensor("slot_table", [SLOTS, 2], F32, kind="Internal").ap()

    with ExitStack() as ctx:
        def sem(name):
            return Counter(ctx.enter_context(nc.semaphore(name)))

        def sb(name, shape, dt=F32, c=None):
            return (c or ctx).enter_context(nc.sbuf_tensor(name, shape, dt))

        def ps(name, shape):
            return ctx.enter_context(nc.psum_tensor(name, shape, F32))

        p_score = ps("p_score", [P, 2, 512])
        p_turn = ps("p_turn", [P, 2, 512])
        p_att = ps("p_att", [P, 512])
        p_proj = ps("p_proj", [P, 2, 512])
        p_misc = ps("p_misc", [P, 512])

        token_of = sb("token_of", [P, NR, NX], U32)
        gate_of = sb("gate_of", [P, NR, NX])
        ident = sb("ident", [P, P])
        slot_of = sb("slot_of", [P, TOK // P], U32)
        id_gate = sb("id_gate", [P, TOK // P, 2])

        s_const = sem("s_const")
        s_scatter = sem("s_scatter")
        s_tabin = sem("s_tabin")
        s_dt = sem("s_dt")
        s_store = [sem(f"s_store{i}") for i in range(NT)]
        s_base = [sem(f"s_base{i}") for i in range(NT)]
        s_sum = [sem(f"s_sum{i}") for i in range(XR)]
        s_xnst = [sem(f"s_xnst{i}") for i in range(TPQ)]

        c1 = ctx.enter_context(ExitStack())

        def sb1(name, shape, dt=F32):
            return sb(name, shape, dt, c1)

        wt = sb1("wt", [P, 3, 2, KT, E], F32R)
        bias = sb1("bias", [P, 3, KT])
        wr = sb1("wr", [P, KT, NX])
        wr_parts = sb1("wr_parts", [P, KT, 2, NX], F32R)
        mask = sb1("mask", [P, CH, 3 * TT])
        q_land = sb1("q_land", [96, CH, QT], F32R)
        qn = sb1("qn", [96, QT, CH], F32R)
        ks = [sb1(f"ks{i}", [96, CH, QT], F32R) for i in range(2)]
        stage = sb1("stage", [P, 2, KT, QT], F32R)
        bias_v = sb1("bias_v", [P, E])
        xt = sb1("xt", [P, 2, KT, QT], F32R)
        xn = sb1("xn", [P, TPQ, E])
        res = sb1("res", [P, XR, E])
        prob = sb1("prob", [P, SR, 3 * P])
        row_max = sb1("row_max", [P, 2, NT, QH])
        vsum = sb1("vsum", [P, 2, NT], F32R)
        far_pick = sb1("far_pick", [2 * NT, NT])
        ones2 = sb1("ones2", [P, 2])
        stats = sb1("stats", [P, TPQ, 6])
        moments = sb1("moments", [P, TPQ, 2])
        rstd = sb1("rstd", [P, TPQ])
        veps = sb1("veps", [P, TPQ])
        newton = sb1("newton", [P, TPQ])
        tri = sb1("tri", [P, P], BF16)
        ones_bf = sb1("ones_bf", [P, P], BF16)
        ex_iota = sb1("ex_iota", [P, NX])
        logitT = sb1("logitT", [2 * NX, QT])
        logit = sb1("logit", [P, TPQ, NX])
        logit_lo = sb1("logit_lo", [P, TPQ, NX])
        top = sb1("top", [P, TPQ, 8])
        top_i = sb1("top_i", [P, TPQ, 8], U32)
        top_f = sb1("top_f", [P, TPQ])
        ntop = sb1("ntop", [P, TPQ])
        expl = sb1("expl", [P, TPQ, NX])
        expsum = sb1("expsum", [P, TPQ])
        onehot = sb1("onehot", [P, 2, NX], BF16)
        seen = sb1("seen", [P, 2, NX], BF16)
        pos_junk = sb1("pos_junk", [P, TPQ, NX])
        pos = sb1("pos", [P, TPQ])
        rej = sb1("rej", [P, TPQ])
        slot_f = sb1("slot_f", [P, TPQ])
        probT = sb1("probT", [P, PR, QH * P])
        vn = sb1("vn", [P, 2, NT, P])
        attT = sb1("attT", [P, 4 * P])
        far_e = sb1("far_e", [P, 4 * P])
        neg_max = sb1("neg_max", [P, 2, NT, QH])
        e_out = sb1("e_out", [P, 2, NT, QH])
        row_sum = sb1("row_sum", [P, 2, NT, QH])
        den = sb1("den", [P, 2, NT, QH])
        rden = sb1("rden", [P, 2, NT, QH])
        n_out = sb1("n_out", [P, NT, QH])
        far_rows = sb1("far_rows", [2 * NT, 2, P], F32R)
        far_pick_r = sb1("far_pick_r", [2 * NT, NT], F32R)
        ao = sb1("ao", [P, NT, E])
        late = sb1("late", [P, E])
        stage_v = sb1("stage_v", [P, TPQ, E])

        s_load = sem("s_load")
        s_bv = sem("s_bv")
        s_wraw = [sem(f"s_wraw{i}") for i in range(3)]
        s_pw = sem("s_pw")
        s_aw = sem("s_aw")
        s_dw = sem("s_dw")
        s_tab = sem("s_tab")

        def fill(t, v):
            return pool.do(lambda e: e.memset(t, v), s_const)

        fill(ident[:], 0.0)
        c0 = fill(mask[:], 1.0)
        pool.wait(c0)
        pool.do(lambda e: e.affine_select(out=ident[:], in_=ident[:], compare_op=ALU.not_equal, fill=1.0, base=0,
                                          pattern=[[-1, P]], channel_multiplier=1), s_const)
        c0 = pool.do(lambda e: e.affine_select(out=mask[:], in_=mask[:], compare_op=ALU.is_ge, fill=0.0, base=0,
                                               pattern=[[1, CH], [CH, 3 * TT]], channel_multiplier=-1), s_const)
        pool.wait(c0)
        pool.do(lambda e: e.affine_select(out=mask[:], in_=mask[:], compare_op=ALU.is_gt, fill=0.0, base=2 * BAND,
                                          pattern=[[-1, CH], [-CH, 3 * TT]], channel_multiplier=1), s_const)
        fill(ones2[:], 1.0)
        fill(ones_bf[:], 1.0)
        c0 = fill(tri[:], 1.0)
        pool.wait(c0)
        pool.do(lambda e: e.affine_select(out=tri[:], in_=tri[:], compare_op=ALU.is_ge, fill=0.0, base=0,
                                          pattern=[[1, P]], channel_multiplier=-1), s_const)
        pool.do(lambda e: e.iota(ex_iota[:], pattern=[[1, NX]], base=0, channel_multiplier=0,
                                 allow_small_or_imprecise_dtypes=True), s_const)
        pool.do(lambda e: e.iota(id_gate[:, :, 0], pattern=[[P, TOK // P]], base=0, channel_multiplier=1,
                                 allow_small_or_imprecise_dtypes=True), s_const)
        c0 = fill(n_out[:], float(S - 3 * P))
        pool.wait(c0)
        fill(n_out[:, 0, :], float(S - 2 * P))
        fill(n_out[:, NT - 1, :], float(S - 2 * P))
        c0 = fill(far_pick[:], 1.0)

        def pick(base, step, fill_value):
            nonlocal c0
            pool.wait(c0)
            c0 = pool.do(lambda e: e.affine_select(out=far_pick[:], in_=far_pick[:], compare_op=ALU.not_equal,
                                                   fill=fill_value, base=base, pattern=[[step, NT]],
                                                   channel_multiplier=-1), s_const)

        for off in (-1, 0, 1, NT - 1, NT, NT + 1):
            pick(off, 1, 0.0)
        pick(NT - 1, -1000, 1.0)
        pick(NT + 1000 * (NT - 1), -1000, 1.0)
        table_init = prob[:, 0, 0:2 * SLOTS // P].rearrange("p (n two) -> p n two", two=2)
        fill(table_init[:, :, 0], FAR)
        c_const = fill(table_init[:, :, 1], 0.0)
        def clear_table():
            sp.wait(c_const)
            return sp.do(lambda e: e.dma_start(slot_table.rearrange("(p n) two -> p (n two)", p=P),
                                                prob[:, 0, 0:2 * SLOTS // P]), s_tab, 16)

        dve.wait(c_const)
        c_pick = dve.do(lambda e: e.tensor_copy(far_pick_r[:], far_pick[:]), s_dw)

        s_x = [sem(f"s_x{i}") for i in range(XR)]
        misc_free = []
        res_free = [[] for _ in range(XR)]
        ao_free = [[] for _ in range(NT)]
        late_free = [[] for _ in range(LR)]
        m_x, m_ln, m_xadd, m_xnst, m_sum, m_rstd = {}, {}, {}, {}, {}, {}

        def load_x(tt):
            sp.wait(*res_free[tt % XR])
            m_x[tt] = sp.do(lambda e: e.dma_start(res[:, tt % XR, :], x_rows[tt * P:(tt + 1) * P, :]),
                            s_x[tt % XR], 16)

        for tt in range(TPQ):
            load_x(tt)

        raw = [vn[:].rearrange("p a t c -> p (a t c)"), ao[:, 0:4, :].rearrange("p t e -> p (t e)"),
               ao[:, 4:8, :].rearrange("p t e -> p (t e)")]
        m_w = []
        for i, (w, b) in enumerate(((Wq, bq), (Wk, bk), (Wv, bv))):
            dst = raw[i].rearrange("p (t e) -> p t e", t=KT)
            sp.do(lambda e, dst=dst, w=w: e.dma_start(dst, w.rearrange("(t p) e -> p t e", p=P)), s_wraw[i], 16)
            m_w.append(sp.do(lambda e, i=i, b=b: e.dma_start(bias[:, i, :], b.rearrange("(t p) -> p t", p=P),
                                                             allow_slow_non_contiguous=True), s_wraw[i], 16))
        m_bv = sp.do(lambda e: e.dma_start(bias_v[:], bv.unsqueeze(0).broadcast_to([P, E])), s_bv, 16)
        m_wr = sp.do(lambda e: e.dma_start(wr[:], w_router.rearrange("(k p) n -> p k n", p=P)), s_load, 16)
        m_tab = clear_table()

        def split_router():
            dve.wait(m_wr)
            c = dve.do(lambda e: e.tensor_copy(wr_parts[:, :, 0, :], wr[:]), s_dw)
            dve.wait(c)
            return dve.do(lambda e: e.tensor_tensor(wr_parts[:, :, 1, :], wr[:], wr_parts[:, :, 0, :].bitcast(F32),
                                                    ALU.subtract), s_dw)

        turn_banks = [p_turn[:, 0, :], p_turn[:, 1, :], p_score[:, 0, :], p_score[:, 1, :]]
        turn_banks_free = [[] for _ in turn_banks]
        m_weights = [[], [], []]

        def turn_weights(i):
            pe.wait(c_const, m_w[i])
            src = raw[i].rearrange("p (t e) -> p t e", t=KT)
            for k in range(KT):
                bank = turn_banks[k]
                pe.wait(*turn_banks_free[k])
                for f in range(KT):
                    m = pe.do(lambda e, f=f, k=k, bank=bank: e.transpose(
                        bank[:, f * P:(f + 1) * P], src[:, f, k * P:(k + 1) * P], ident[:]),
                        s_pw if f == KT - 1 else None)
                act.wait(m)
                a = act.do(lambda e, k=k, bank=bank: e.activation(wt[:, i, 0, k, :], bank, ACT.Copy), s_aw)
                dve.wait(m, a)
                d = dve.do(lambda e, k=k, bank=bank: e.tensor_tensor(
                    wt[:, i, 1, k, :], bank, wt[:, i, 0, k, :].bitcast(F32), ALU.subtract), s_dw)
                turn_banks_free[k] = [a, d]
                m_weights[i] += [a, d]

        s_q = [sem(f"s_q{i}") for i in range(3)]
        s_k = [[sem(f"s_k{i}{j}") for j in range(3)] for i in range(2)]
        s_vst = sem("s_vst")
        s_v = [sem(f"s_v{i}") for i in range(2)]
        s_copy = sem("s_copy")
        s_ln = sem("s_ln")
        s_newton = sem("s_newton")
        s_resadd = sem("s_resadd")
        s_xturn = sem("s_xturn")
        s_xhi = sem("s_xhi")
        s_xlo = sem("s_xlo")
        s_proj = sem("s_proj")
        s_phi = sem("s_phi")
        s_plo = sem("s_plo")
        s_score = sem("s_score")
        s_masked = sem("s_masked")
        s_negm = sem("s_negm")
        s_exp = sem("s_exp")
        s_turn = sem("s_turn")
        s_turnedA = sem("s_turned_act")
        s_turnedD = sem("s_turned_dve")
        s_pv = sem("s_pv")
        s_att = sem("s_att")
        s_post = sem("s_post")
        s_norm = sem("s_norm")
        s_pm = sem("s_pm")
        s_ma = sem("s_ma")
        s_md = sem("s_md")
        s_rt = sem("s_rt")
        s_resdone = sem("s_resdone")
        s_late = [sem(f"s_late{i}") for i in range(LR)]

        def norm_stats(tt):
            j, r = tt % TPQ, tt % XR
            dve.wait(m_x[tt])
            if tt >= TPQ:
                dve.wait(m_ln[tt - TPQ])
            c = dve.do(lambda e: e.bn_stats(stats[:, j, :], res[:, r, :]), s_ln)
            dve.wait(c)
            m_moments[tt] = dve.do(lambda e: e.bn_aggr(moments[:, j, :], stats[:, j, :]), s_ln)

        m_moments = {}

        def norm_scale(q):
            dve.wait(*[m_moments[q * TPQ + t] for t in range(TPQ)])
            if q:
                dve.wait(m_rstd[q - 1])
            c = dve.do(lambda e: e.tensor_scalar(veps[:], moments[:, :, 1], 1e-5, None, ALU.add), s_ln)
            dve.wait(c)
            if q:
                dve.wait(m_ln[q * TPQ - 1])
            c = dve.do(lambda e: e.tensor_scalar(rstd[:].bitcast(I32), veps[:].bitcast(I32), -0.5,
                                                 float(0x5F3759DF), ALU.mult, ALU.add), s_ln)

            def step(emit):
                nonlocal c
                pool.wait(c)
                c = pool.do(emit, s_newton)

            for _ in range(3):
                step(lambda e: e.tensor_tensor(newton[:], rstd[:], rstd[:], ALU.mult))
                step(lambda e: e.tensor_tensor(newton[:], newton[:], veps[:], ALU.mult))
                step(lambda e: e.tensor_scalar(newton[:], newton[:], -0.5, 1.5, ALU.mult, ALU.add))
                step(lambda e: e.tensor_tensor(rstd[:], rstd[:], newton[:], ALU.mult))
            m_rstd[q] = c

        def layer_norm(tt):
            j, r = tt % TPQ, tt % XR
            dve.wait(m_rstd[tt // TPQ])
            if tt >= TPQ:
                dve.wait(m_xturn[tt - TPQ], m_xnst[tt - TPQ], m_xadd[tt - TPQ])
            m_ln[tt] = dve.do(lambda e: e.tensor_scalar(xn[:, j, :], res[:, r, :], moments[:, j, 0:1],
                                                        rstd[:, j:j + 1], ALU.subtract, ALU.mult), s_ln)
            pool.wait(m_ln[tt])
            m_xadd[tt] = pool.do(lambda e: e.tensor_tensor(res[:, r, :], res[:, r, :], xn[:, j, :], ALU.add),
                                 s_resadd)
            sp.wait(m_ln[tt])
            sp.wait(m_xadd[tt])
            m_sum[tt] = sp.do(lambda e: e.dma_start(sum_rows[tt * P:(tt + 1) * P, :], res[:, r, :]), s_sum[r], 16)
            res_free[r] = [m_sum[tt]]
            m_xnst[tt] = sp.do(lambda e: e.dma_start(xn_rows[tt * P:(tt + 1) * P, :], xn[:, j, :]), s_xnst[j], 16)

        m_xturn, m_xparts = {}, {}
        proj_free = [[], []]
        n_proj = 0

        def turn_x(tt):
            nonlocal n_proj
            j = tt % TPQ
            bank = n_proj % 2
            n_proj += 1
            pe.wait(m_ln[tt], *proj_free[bank])
            proj_free[bank] = None
            for k in range(KT):
                m = pe.do(lambda e, k=k: e.transpose(p_proj[:, bank, k * P:(k + 1) * P],
                                                     xn[:, j, k * P:(k + 1) * P], ident[:]),
                          s_xturn if k == KT - 1 else None)
            m_xturn[tt] = m

            def take():
                src = p_proj[:, bank, :].rearrange("p (k t) -> p k t", k=KT)
                act.wait(m)
                if tt >= TPQ:
                    act.wait(last_proj[tt // TPQ - 1])
                a = act.do(lambda e: e.activation(xt[:, 0, :, j * P:(j + 1) * P], src, ACT.Copy), s_xhi)
                dve.wait(a)
                d = dve.do(lambda e: e.tensor_tensor(xt[:, 1, :, j * P:(j + 1) * P], src,
                                                     xt[:, 0, :, j * P:(j + 1) * P].bitcast(F32), ALU.subtract), s_xlo)
                proj_free[bank] = [a, d]
                m_xparts[tt] = [a, d]

            return take

        last_proj = {}
        rt = {}

        def router_products(q):
            nonlocal misc_free
            pe.wait(m_wrp, *[m for t in range(TPQ) for m in m_xparts[q * TPQ + t]], *misc_free)
            terms = [(k, a) for k in range(KT) for a in (0, 1)]
            for n, (k, a) in enumerate(terms):
                m = pe.do(lambda e, n=n, k=k, a=a: e.matmul(
                    p_misc[0:2 * NX, 0:QT], wr_parts[:, k].rearrange("p a n -> p (a n)"), xt[:, a, k, :],
                    start=n == 0, stop=n == len(terms) - 1), s_pm if n == len(terms) - 1 else None)
            last_proj[q] = m
            misc_free = None

            def take():
                nonlocal misc_free
                act.wait(m)
                a = act.do(lambda e: e.activation(logitT[:], p_misc[0:2 * NX, 0:QT], ACT.Copy), s_ma)
                misc_free = [a]
                rt["T"] = a

            return take

        def rstep(emit, *marks):
            dve.wait(*marks)
            return dve.do(emit, s_rt)

        def route_turn(q):
            nonlocal misc_free
            pe.wait(rt["T"], *misc_free)
            for t in range(TPQ):
                m = pe.do(lambda e, t=t: e.transpose(p_misc[:, t * 2 * NX:(t + 1) * 2 * NX],
                                                     logitT[:, t * P:(t + 1) * P], ident[0:2 * NX, 0:2 * NX]), s_pm)
            misc_free = None

            def take():
                nonlocal misc_free
                both = p_misc[:, 0:TPQ * 2 * NX].rearrange("p (t a n) -> p t a n", t=TPQ, a=2)
                c = rstep(lambda e: e.tensor_copy(logit_lo[:], both[:, :, 1, :]), m)
                c = rstep(lambda e: e.tensor_tensor(logit[:], both[:, :, 0, :], logit_lo[:], ALU.add), c,
                          *rt.get("exp", []))
                misc_free = [c]
                rt["logit"] = c

            return take

        def choose(q):
            for t in range(TPQ):
                c = rstep(lambda e, t=t: e.max(top[:, t], logit[:, t, :]), rt["logit"])
            n = rstep(lambda e: e.tensor_scalar(ntop[:], top[:, :, 0], -1.0, None, ALU.mult), c, *rt.get("exp", []))
            for t in range(TPQ):
                c = rstep(lambda e, t=t: e.max_index(top_i[:, t], top[:, t], logit[:, t, :]))
            act.wait(n)
            if q:
                act.wait(rt["gate"])
            for t in range(TPQ):
                a = act.do(lambda e, t=t: e.activation(expl[:, t], logit[:, t, :], ACT.Exp, bias=ntop[:, t:t + 1],
                                                       accum_out=expsum[:, t:t + 1]), s_ma)
            rt["exp"] = [a]
            c = rstep(lambda e: e.tensor_copy(top_f[:], top_i[:, :, 0]), c)
            for t in range(TPQ):
                rt["onehot"] = rstep(lambda e, t=t: e.tensor_scalar(
                    onehot[:, t, :], ex_iota[:], top_f[:, t:t + 1], None, ALU.is_equal), c, c_const,
                    *rt.get("counted", []))

        def place(q):
            nonlocal misc_free
            new = q % 2
            pe.wait(rt["onehot"], *misc_free)
            if q:
                pe.wait(rt["seen"])
            for t in range(TPQ):
                cols = slice(t * NX, (t + 1) * NX)
                terms = ([(ones_bf, seen[:, 1 - new, :])] if q else []) + \
                    [(ones_bf, onehot[:, u, :]) for u in range(t)] + [(tri, onehot[:, t, :])]
                for i, (w_, v_) in enumerate(terms):
                    m = pe.do(lambda e, i=i, w_=w_, v_=v_, cols=cols, n=len(terms): e.matmul(
                        p_misc[:, cols], w_[:], v_, start=i == 0, stop=i == n - 1), s_pm)
            rt["counted"] = [m]
            misc_free = None

            def take():
                nonlocal misc_free
                if q:
                    c = rstep(lambda e: e.tensor_tensor(seen[:, new, :], seen[:, 1 - new, :], onehot[:, 0, :], ALU.add))
                else:
                    c = rstep(lambda e: e.tensor_copy(seen[:, new, :], onehot[:, 0, :]), rt["onehot"])
                for t in range(1, TPQ):
                    c = rstep(lambda e, t=t: e.tensor_tensor(seen[:, new, :], seen[:, new, :], onehot[:, t, :],
                                                             ALU.add), c)
                rt["seen"] = c
                for t in range(TPQ):
                    c = rstep(lambda e, t=t: e.tensor_tensor_reduce(
                        pos_junk[:, t], onehot[:, t, :], p_misc[:, t * NX:(t + 1) * NX], 1.0, 0.0, ALU.mult, ALU.add,
                        pos[:, t:t + 1]), m)
                misc_free = [c]
                tiles = slice(q * TPQ, (q + 1) * TPQ)
                rstep(lambda e: e.tensor_scalar(rej[:], pos[:], float(CAP), FAR, ALU.is_gt, ALU.mult), c)
                c = rstep(lambda e: e.scalar_tensor_tensor(out=slot_f[:], in0=top_f[:], scalar=float(CAP),
                                                           in1=pos[:], op0=ALU.mult, op1=ALU.add))
                c = rstep(lambda e: e.scalar_tensor_tensor(out=slot_of[:, tiles], in0=slot_f[:], scalar=-1.0,
                                                           in1=rej[:], op0=ALU.add, op1=ALU.add), c)
                rt["gate"] = rstep(lambda e: e.reciprocal(id_gate[:, tiles, 1], expsum[:]), *rt["exp"])
                pool.wait(c, rt["gate"], m_tab)
                for tt in range(q * TPQ, (q + 1) * TPQ):
                    pool.do(lambda e, tt=tt: e.indirect_dma_start(
                        out=slot_table[:, :], out_offset=bass.IndirectOffsetOnAxis(ap=slot_of[:, tt:tt + 1], axis=0),
                        in_=id_gate[:, tt, :], in_offset=None, bounds_check=SLOTS - 1, oob_is_err=False), s_scatter, 16)

            return take

        m_q, m_k = {}, {}

        def project(q, n, f):
            nonlocal n_proj
            which = n
            r = n_proj % 2
            n_proj += 1
            pe.wait(*m_weights[which], *[m for t in range(TPQ) for m in m_xparts[q * TPQ + t]], *proj_free[r])
            terms = [(k, a, b) for k in range(KT) for a, b in ((0, 0), (0, 1), (1, 0))]
            for i, (k, a, b) in enumerate(terms):
                m = pe.do(lambda e, i=i, k=k, a=a, b=b: e.matmul(
                    p_proj[:, r, 0:QT], wt[:, which, a, k, f * P:(f + 1) * P], xt[:, b, k, :],
                    start=i == 0, stop=i == len(terms) - 1), s_proj if i == len(terms) - 1 else None)
            last_proj[q] = m
            proj_free[r] = None

            def take():
                act.wait(m, m_w[which], *stage_free[f // 2])
                b = bias[:, which, f:f + 1]
                hi = stage[:, 0, f, :]
                a = act.do(lambda e: e.activation(hi, p_proj[:, r, 0:QT], ACT.Identity, bias=b), s_phi)
                dve.wait(a)
                d = dve.do(lambda e: e.scalar_tensor_tensor(out=stage[:, 1, f, :], in0=p_proj[:, r, 0:QT], scalar=b,
                                                            in1=hi.bitcast(F32), op0=ALU.add, op1=ALU.subtract), s_plo)
                proj_free[r] = [d]
                if f % 2 == 1:
                    sp.wait(d)
                    move(q, which, f // 2)

            return take

        def project_v(q, t):
            nonlocal n_proj
            r = n_proj % 2
            n_proj += 1
            pe.wait(*m_weights[2], *[m for u in range(TPQ) for m in m_xparts[q * TPQ + u]], *proj_free[r])
            terms = [(k, a, b) for k in range(KT) for a, b in ((0, 0), (0, 1), (1, 0))]
            for i, (k, a, b) in enumerate(terms):
                m = pe.do(lambda e, i=i, k=k, a=a, b=b: e.matmul(
                    p_proj[:, r, :], xt[:, a, k, t * P:(t + 1) * P], wt[:, 2, b, k, :],
                    start=i == 0, stop=i == len(terms) - 1), s_proj if i == len(terms) - 1 else None)
            last_proj[q] = m
            proj_free[r] = None

            def take(m=m):
                dve.wait(m, m_bv, *stage_v_free)
                d = dve.do(lambda e: e.tensor_tensor(stage_v[:, t, :], p_proj[:, r, :], bias_v[:], ALU.add), s_plo)
                proj_free[r] = [d]
                if t < TPQ - 1:
                    return
                sp.wait(d)
                m = sp.do(lambda e: e.dma_start(v_rows[q * QT:(q + 1) * QT, :].rearrange("(t p) e -> p t e", p=P),
                                                stage_v[:]), s_vst, 16)
                stage_v_free[:] = [m]
                m_vstored[q] = m

            return take

        m_vstored = {}

        def fetch_v(q):
            sp.wait(m_vstored[q])
            if q >= 2:
                sp.wait(m_pv[(q - 2) * NT + NT - 1], m_vread[q - 2])
            heads = v_rows[q * QT:(q + 1) * QT, :].rearrange("(g t) (c d) -> g (t c) d", g=QH, d=D)
            for g in range(QH):
                m = sp.do(lambda e, g=g: e.dma_start(vn[:, q % 2, :, g * D:(g + 1) * D],
                                                     heads[g].rearrange("(n p) d -> p n d", p=P)), s_v[q % 2], 16)
            m_vn[q] = m

        stage_free, stage_v_free, q_land_free = [[], []], [], []

        def landing(q, which):
            return (q_land, s_q, m_q, 0, 1, 2) if which == 0 else (ks[q % 2], s_k[q % 2], m_k, 0, 2, 1)

        def move(q, which, half):
            dst, landed, marks, hi_row, lo_row, _ = landing(q, which)
            if which == 0:
                sp.wait(*q_land_free)
            elif q >= 2:
                sp.wait(m_scored[(q - 2) * NT + NT - 1])
            for part, row in enumerate((hi_row, lo_row)):
                for c4 in range(4):
                    m = sp.do(lambda e, row=row, part=part, c4=c4: e.dma_start(
                        dst[row * D:(row + 1) * D, 8 * half + c4:8 * half + c4 + 5:4, :].bitcast(F32),
                        stage[c4 * D:(c4 + 1) * D, part, 2 * half:2 * half + 2, :].bitcast(F32)), landed[half], 16)
            stage_free[half] = [m]
            marks.setdefault(q, []).append(m)

        def double(q, which):
            dst, landed, marks, hi_row, _, again = landing(q, which)
            sp.wait(*marks[q])
            marks[q].append(sp.do(lambda e: e.dma_start(dst[again * D:(again + 1) * D, :, :].bitcast(F32),
                                                   dst[hi_row * D:(hi_row + 1) * D, :, :].bitcast(F32)),
                                  landed[2], 16))

        m_qcopy, m_scored = {}, {}

        def copy_q(q, j):
            pool.wait(*m_q[q])
            if q:
                pool.wait(m_scored[(q - 1) * NT + 2 * j + 1])
            w = 2 * TT
            src = q_land[:].bitcast(F32).rearrange("p c (g t) -> p g t c", g=QH)
            dst = qn[:].rearrange("p (g t) c -> p g t c", g=QH)
            m_qcopy[q, j] = pool.do(lambda e: e.tensor_copy(dst[:, :, j * w:(j + 1) * w, :],
                                                            src[:, :, j * w:(j + 1) * w, :]), s_copy)
            if j == 3:
                q_land_free[:] = [m_qcopy[q, j]]

        m_vn, m_far, m_vread = {}, {}, {}

        def far_sums(q):
            nonlocal misc_free
            par = q % 2
            pe.wait(m_vn[q], *misc_free)
            for t in range(NT):
                m = pe.do(lambda e, t=t: e.matmul(p_misc[:, 2 * t:2 * t + 2], vn[:, par, t, :], ones2[:], start=True,
                                                  stop=True), s_pm if t == NT - 1 else None)
            m_vread[q] = m
            misc_free = None

            def take():
                nonlocal misc_free
                src = p_misc[:, 0:2 * NT].rearrange("p (t two) -> p t two", two=2)[:, :, 0]
                dve.wait(m)
                c = dve.do(lambda e: e.tensor_copy(vsum[:, 0, :], src), s_md)
                dve.wait(c)
                c = dve.do(lambda e: e.tensor_tensor(vsum[:, 1, :], src, vsum[:, 0, :].bitcast(F32), ALU.subtract),
                           s_md)
                misc_free = [c]
                m_vsum[q] = c

            return take

        m_vsum = {}

        def far_sums_turn(q):
            nonlocal misc_free
            pe.wait(m_vsum[q], *misc_free)
            m = pe.do(lambda e: e.transpose(p_misc[0:2 * NT, 0:P],
                                            vsum[:].rearrange("p a t -> p (a t)").bitcast(F32), ident[:]), s_pm)
            misc_free = None

            def take():
                nonlocal misc_free
                act.wait(m)
                a = act.do(lambda e: e.activation(far_rows[:, q % 2, :], p_misc[0:2 * NT, 0:P], ACT.Copy), s_ma)
                misc_free = [a]
                m_far[q] = a

            return take

        score_free = [[], []]
        prob_free = [[] for _ in range(SR)]
        prob_free[0] = [m_tab]
        m_exp, m_eout, m_row_free = {}, {}, {}
        n_score = 0

        def window(T):
            first = max(T - 1, 0)
            return first, min(T + 2, NT) - first

        def scores(s, g):
            nonlocal n_score
            q, T = divmod(s, NT)
            par = q % 2
            first, nj = window(T)
            w = nj * TT
            m_lo = 0 if T else TT
            r = n_score % 2
            slot = n_score % SR
            n_score += 1
            row = g * HT
            pe.wait(m_qcopy[q, T // 2], *m_k[q], *score_free[r])
            score_free[r] = None
            slots_of.setdefault(s, []).append(slot)
            m = pe.do(lambda e: e.matmul(
                p_score[:, r, 0:CH * w],
                qn[:, row + T * TT:row + (T + 1) * TT, :].rearrange("p t c -> p (t c)"),
                ks[par][:, :, row + first * TT:row + first * TT + w], start=True, stop=True), s_score)
            m_scored[s] = m

            def take():
                dve.wait(m, c_const, *prob_free[slot])
                if g == 0 and q >= 2:
                    dve.wait(m_row_free[q - 2])
                d = dve.do(lambda e: e.tensor_tensor_reduce(
                    prob[:, slot, 0:CH * w].rearrange("p (t c) -> p c t", c=CH),
                    p_score[:, r, 0:CH * w].rearrange("p (c t) -> p c t", c=CH),
                    mask[:, :, m_lo:m_lo + w], 1.0, 0.0, ALU.mult, ALU.max, row_max[:, par, T, g:g + 1]), s_masked)
                score_free[r] = [d]

            return take

        slots_of = {}

        def weights(s, pair):
            q, T = divmod(s, NT)
            par = q % 2
            w = window(T)[1] * TT
            two = slice(2 * pair, 2 * pair + 2)
            dve.wait((s_masked, s_masked.value))
            c = dve.do(lambda e: e.tensor_scalar(neg_max[:, par, T, two], row_max[:, par, T, two], -SCALE, None,
                                                 ALU.mult), s_negm)

            def exps():
                act.wait(c)
                for g in (2 * pair, 2 * pair + 1):
                    slot = slots_of[s][g]
                    a = act.do(lambda e, g=g, slot=slot: e.activation(
                        prob[:, slot, 0:CH * w], prob[:, slot, 0:CH * w], ACT.Exp, bias=neg_max[:, par, T, g:g + 1],
                        scale=SCALE, accum_out=row_sum[:, par, T, g:g + 1]), s_exp)
                if pair == 1:
                    m_exp[s] = (a, slots_of[s])
                    m_eout[s] = act.do(lambda e: e.activation(e_out[:, par, T, :], neg_max[:, par, T, :], ACT.Exp),
                                       s_exp)
            return exps

        turn_free = [[], []]
        n_turn = 0
        m_probT, m_pv, turn_step, place_of = {}, {}, {}, {}

        def turn_probs(s, jj):
            nonlocal n_turn
            q, T = divmod(s, NT)
            first, nj = window(T)
            if jj >= nj:
                return
            n, n_turn = n_turn, n_turn + 1
            r = n % 2
            mark, slots = m_exp[s]
            pe.wait(mark, *turn_free[r])
            turn_free[r] = None
            turn_step[n] = s
            place_of[s, jj] = n % PR
            for g, slot in enumerate(slots):
                m = pe.do(lambda e, g=g, slot=slot: e.transpose(
                    p_turn[:, r, g * P:(g + 1) * P], prob[:, slot, jj * P:(jj + 1) * P], ident[:]),
                    s_turn if g == QH - 1 else None)
            if jj == nj - 1:
                for slot in slots:
                    prob_free[slot] = [m]

            def take():
                eng, cnt = (dve, s_turnedD) if jj == 1 else (act, s_turnedA)
                eng.wait(m)
                if n >= PR:
                    eng.wait(m_pv[turn_step[n - PR]])
                dst = probT[:, n % PR, :]
                if eng is act:
                    a = act.do(lambda e: e.activation(dst, p_turn[:, r, :], ACT.Copy), cnt)
                else:
                    a = dve.do(lambda e: e.tensor_copy(dst, p_turn[:, r, :]), cnt)
                turn_free[r] = [a]
                m_probT.setdefault(s, []).append(a)

            return take

        att_free = []

        def weigh(s):
            q, T = divmod(s, NT)
            par = q % 2
            first, nj = window(T)
            pe.wait(m_vn[q], *m_probT[s], *(att_free if T % 4 == 0 else []))
            col = (T % 4) * P
            for jj in range(nj):
                for g in range(QH):
                    m = pe.do(lambda e, jj=jj, g=g: e.matmul(
                        p_att[g * D:(g + 1) * D, col:col + P], vn[:, par, first + jj, g * D:(g + 1) * D],
                        probT[:, place_of[s, jj], g * P:(g + 1) * P], start=jj == 0, stop=jj == nj - 1,
                        skip_group_check=True), s_pv if jj == nj - 1 and g == QH - 1 else None)
            m_pv[s] = m

        m_addend = {}

        def far_part(s):
            nonlocal misc_free, att_free
            q, T = divmod(s, NT)
            half, par = T // 4, q % 2
            t0 = half * 4
            act.wait(m_pv[s])
            if m_addend:
                act.wait(m_addend["attT"])
            a = act.do(lambda e: e.activation(attT[:], p_att[:], ACT.Copy), s_att)
            att_free = [a]
            pe.wait(m_far[q], c_pick, *misc_free)
            for t in range(4):
                m = pe.do(lambda e, t=t: e.matmul(
                    p_misc[:, t * P:(t + 1) * P], far_pick_r[:, t0 + t:t0 + t + 1].broadcast_to([2 * NT, P]),
                    far_rows[:, par, :], start=True, stop=True), s_pm if t == 3 else None)
            m_far_sum[s] = (a, m)
            misc_free = None

        m_far_sum = {}

        def far_weigh(s):
            nonlocal misc_free
            q, T = divmod(s, NT)
            half, par = T // 4, q % 2
            t0 = half * 4
            a, m = m_far_sum[s]
            eo = e_out[:, par, t0:t0 + 4, :].rearrange("p t g -> p (t g)")
            tg = 4 * QH

            def wide(v):
                return v.unsqueeze(2).broadcast_to([P, tg, D])

            def cols(v):
                return v.rearrange("p (n d) -> p n d", d=D)

            dve.wait(m, m_eout[s], *m_addend.get("far_e", []))
            d = dve.do(lambda e: e.tensor_tensor(cols(far_e[:]), cols(p_misc[:]), wide(eo), ALU.mult), s_post)
            misc_free = [d]
            den_v = den[:, par, t0:t0 + 4, :].rearrange("p t g -> p (t g)")
            rden_v = rden[:, par, t0:t0 + 4, :].rearrange("p t g -> p (t g)")
            c = dve.do(lambda e: e.tensor_tensor(den_v, n_out[:, t0:t0 + 4, :].rearrange("p t g -> p (t g)"), eo,
                                                 ALU.mult), s_post)
            dve.wait(c)
            c = dve.do(lambda e: e.tensor_tensor(den_v, den_v, row_sum[:, par, t0:t0 + 4, :].rearrange(
                "p t g -> p (t g)"), ALU.add), s_post)
            dve.wait(c)
            c = dve.do(lambda e: e.reciprocal(rden_v, den_v), s_post)
            m_far_e[s] = (a, d, c)

        m_far_e = {}

        def finish(s):
            nonlocal misc_free
            q, T = divmod(s, NT)
            half, par = T // 4, q % 2
            t0 = half * 4
            a, d, c = m_far_e[s]

            def cols(v):
                return v.rearrange("p (n d) -> p n d", d=D)

            pe.wait(a, *misc_free)
            for t in range(4):
                m = pe.do(lambda e, t=t: e.transpose(p_misc[:, t * P:(t + 1) * P], attT[:, t * P:(t + 1) * P],
                                                     ident[:]), s_pm if t == 3 else None)
            m_addend["attT"] = m
            misc_free = None

            def take(d=d):
                nonlocal misc_free
                dve.wait(m, d)
                d = dve.do(lambda e: e.tensor_tensor(far_e[:], p_misc[:], far_e[:], ALU.add), s_post)
                misc_free = [d]
                b, qd = divmod(q, QB)
                pool.wait(d, c)
                if qd == 0:
                    for t in range(4):
                        pool.wait(*ao_free[t0 + t])
                for_t = ao[:, t0:t0 + 4, qd * P:(qd + 1) * P].rearrange("p t (g d) -> p t g d", d=D)
                tiles = far_e[:].rearrange("p (t g d) -> p t g d", t=4, g=QH)
                rd = rden[:, par, t0:t0 + 4, :]
                for t in range(4):
                    d = pool.do(lambda e, t=t: e.tensor_tensor(
                        for_t[:, t], tiles[:, t], rd[:, t].unsqueeze(2).broadcast_to([P, QH, D]), ALU.mult), s_norm)
                m_addend["far_e"] = [d]
                if half == 1:
                    m_row_free[q] = d
                if qd == QB - 1:
                    late_jobs.extend((b, t0 + t, d) for t in range(4))

            return take

        late_jobs, late_stage = [], []
        late_place = [late[:], stage_v[:, 0, :], stage_v[:, 1, :]]
        n_late = 0

        def late_load():
            nonlocal n_late
            if not late_jobs:
                return
            b, t, done = late_jobs.pop(0)
            tt = b * NT + t
            r = n_late % LR if b == B - 1 else 0
            n_late += 1
            sp.wait(m_sum[tt], *late_free[r], *(stage_v_free if r else []))
            m = sp.do(lambda e: e.dma_start(late_place[r], sum_rows[tt * P:(tt + 1) * P, :]), s_late[r], 16)
            late_stage.append((t, tt, r, m, done))

        def late_add(ahead):
            if len(late_stage) < (ahead if late_jobs else 1):
                return
            t, tt, r, m, done = late_stage.pop(0)
            pool.wait(m, done)
            m = pool.do(lambda e: e.tensor_tensor(ao[:, t, :], ao[:, t, :], late_place[r], ALU.add), s_resdone)
            late_free[r] = [m]
            return t, tt, m

        def late_store(job):
            if not job:
                return
            t, tt, m = job
            sp.wait(m)
            m1 = sp.do(lambda e: e.dma_start(out_rows[tt * P:(tt + 1) * P, :], ao[:, t, :]), s_store[t], 16)
            m2 = sp.do(lambda e: e.dma_start(base_rows[tt * P:(tt + 1) * P, :], ao[:, t, :]), s_base[t], 16)
            ao_free[t] = [m1, m2]

        for tt in range(TPQ):
            norm_stats(tt)
        norm_scale(0)
        for tt in range(TPQ):
            layer_norm(tt)
            load_x(tt + TPQ)
        turn_weights(0)
        for tt in range(TPQ):
            turn_x(tt)()
        for f in range(KT):
            project(0, 0, f)()
        double(0, 0)
        turn_weights(1)
        for f in range(KT):
            project(0, 1, f)()
        double(0, 1)
        turn_weights(2)
        ao_free = [m_weights[1] + m_weights[2]] * NT
        m_wrp = split_router()
        for tt in range(TPQ, 2 * TPQ):
            norm_stats(tt)
        norm_scale(1)
        for tt in range(TPQ, 2 * TPQ):
            layer_norm(tt)
            load_x(tt + TPQ)
        copy_q(0, 0)
        for t in range(TPQ):
            project_v(0, t)()
        sp.wait(*m_weights[0])
        fetch_v(0)
        router_products(0)()
        for tt in range(TPQ, 2 * TPQ):
            turn_x(tt)()
        route_turn(0)()
        choose(0)
        place(0)()
        for j in range(1, 4):
            copy_q(0, j)
        score_free = [turn_banks_free[2], turn_banks_free[3]]
        turn_free = [turn_banks_free[0], turn_banks_free[1]]
        NS = NQ * NT
        CHUNKS = [
            [("q", 0), ("q", 1)],
            [("q", 2), ("q", 3)],
            [("k", 0), ("k", 1)],
            [("k", 2), ("k", 3)],
            [None, None],
            [("v", 0), None],
            [("v", 1), None],
            [None, None],
        ]

        def chunk(q, T, n):
            if q + 1 < NQ and CHUNKS[T][n]:
                what, part = CHUNKS[T][n]
                if what == "v":
                    return project_v(q + 1, part)
                return project(q + 1, "qk".index(what), part)

        def misc(s, n):
            q, T = divmod(s, NT)
            here, ahead, after = q < NQ, q + 1 < NQ, 0 < q <= NQ
            job = MISC[T][n]
            if job == "products" and ahead:
                return router_products(q + 1)
            if job == "route" and ahead:
                return route_turn(q + 1)
            if job == "place" and ahead:
                return place(q + 1)
            if job == "sums" and here:
                return far_sums(q)
            if job == "sums_turn" and here:
                return far_sums_turn(q)
            if job == "far" and (here if T > 2 else after):
                return far_part(s - 1)
            if job == "finish" and (here if T > 2 else after):
                return finish(s - 2)

        MISC = [
            ["products", "far"],
            ["route", "finish"],
            ["", "sums"],
            ["sums_turn", ""],
            ["place", "far"],
            ["", "finish"],
            ["", ""],
            ["", ""],
        ]

        for pair in (0, 1):
            scores(0, 2 * pair)()
            scores(0, 2 * pair + 1)()
            weights(0, pair)()
        ORDER = (
            "X0 S0 s0 S1 s1 C0 C1 X1 F M0 x0 H "
            "T0 S2 N0 c0 m0 S3 s2 s3 x1 c1 T1 t0 "
            "N1 B n0 t1 n1 P M1 T2 t2 m1"
        ).split()

        def step(s):
            q, T = divmod(s, NT)
            ahead, more = q + 1 < NQ, s + 1 < NS
            if ahead and T == 2:
                double(q + 1, 0)
            if ahead and T == 5:
                double(q + 1, 1)
            if ahead and T == 7:
                fetch_v(q + 1)
            late_sum = late_add(LR if s >= NS else 1)
            late_load()
            held = {}

            def norms():
                if q + 2 < NQ:
                    if T in (0, 1):
                        norm_stats((q + 2) * TPQ + T)
                    if T == 2:
                        norm_scale(q + 2)
                    if T in (3, 4):
                        layer_norm((q + 2) * TPQ + T - 3)

            jobs = {"F": lambda: far_weigh(s - 2) if T == 1 and 0 < q <= NQ or T == 5 and q < NQ else None,
                    "H": lambda: choose(q + 1) if T == 2 and ahead else None,
                    "P": lambda: weigh(s - 1) if 1 <= s <= NS else None,
                    "B": norms}
            for n in range(3):
                jobs[f"T{n}"] = lambda n=n: turn_probs(s, n) if s < NS else None
            for n in range(2):
                jobs[f"C{n}"] = lambda n=n: chunk(q, T, n)
                jobs[f"M{n}"] = lambda n=n: misc(s, n)
                jobs[f"X{n}"] = lambda n=n: turn_x((q + 2) * TPQ + n) if T == 7 and q + 2 < NQ else None
                jobs[f"N{n}"] = lambda n=n: weights(s + 1, n) if more else None
            for g in range(QH):
                jobs[f"S{g}"] = lambda g=g: scores(s + 1, g) if more else None
            for name in ORDER:
                if name.islower():
                    take = held.pop(name.upper())
                    if take:
                        take()
                elif name in ("F", "H", "P", "B"):
                    jobs[name]()
                else:
                    held[name] = jobs[name]()
            assert not held
            if ahead and T in (4, 5, 6, 7):
                copy_q(q + 1, T - 4)
            if T in (5, 6) and q + 3 < NQ:
                load_x((q + 3) * TPQ + T - 5)
            late_store(late_sum)

        tab_rows = q_land[0:NX, :, :].bitcast(F32).rearrange("n c t -> n (c t)")[:, 0:2 * CAP]

        def read_table():
            sp.wait((s_scatter, s_scatter.value))
            sp.wait(*q_land_free)
            return sp.do(lambda e: e.dma_start(tab_rows, slot_table.rearrange("(n c) two -> n (c two)", n=NX)),
                         s_tabin, 16)

        def turn_table(m_tabin):
            nonlocal misc_free
            pe.wait(m_tabin, *misc_free)
            rows = tab_rows.rearrange("n (c two) -> n c two", two=2)
            for r in range(NR):
                for v in range(2):
                    m = pe.do(lambda e, r=r, v=v: e.transpose(
                        p_misc[0:wide_of[r], (2 * r + v) * NX:(2 * r + v + 1) * NX],
                        rows[:, r * P:r * P + wide_of[r], v], ident[0:NX, 0:NX]), s_pm)
            dve.wait(m)
            for r in range(NR):
                w = wide_of[r]
                dve.do(lambda e, r=r, w=w: e.tensor_copy(token_of[0:w, r, :],
                                                         p_misc[0:w, 2 * r * NX:(2 * r + 1) * NX]), s_dt)
                c = dve.do(lambda e, r=r, w=w: e.tensor_copy(gate_of[0:w, r, :],
                                                             p_misc[0:w, (2 * r + 1) * NX:(2 * r + 2) * NX]), s_dt)
            misc_free = [c]
            return c

        for s in range(NS - 1):
            step(s)
            if s == NS - NT:
                m_tabin = read_table()
            if s == NS - 3:
                c_tab = turn_table(m_tabin)

        c1.close()

        RW = 4
        RS = 4
        wraw = sb("wraw", [P, RW, KT, FF])
        xg = sb("xg", [P, 2, NR, E])
        yb = sb("yb", [P, 2, NR, E])
        xe = sb("xe", [P, 2, 2, KT, CAP], F32R)
        wsplit = sb("wsplit", [P, RS, 2, KT, FF], F32R)
        sg = sb("sg", [P, 2, CAP])
        hid = sb("hid", [P, 2, CAP])
        hparts = sb("hparts", [P, 2, KT, CAP], F32R)

        s_clear = sem("s_clear")
        s_wr = [sem(f"s_wr{i}") for i in range(RW)]
        s_whi = sem("s_whi")
        s_wloD = sem("s_wlo_dve")
        s_wloP = sem("s_wlo_pool")
        s_xg = [sem(f"s_xg{i}") for i in range(2)]
        s_yb = [sem(f"s_yb{i}") for i in range(2)]
        s_ys = [sem(f"s_ys{i}") for i in range(2)]
        s_xeP = sem("s_xe_pe")
        s_xeA = sem("s_xe_act")
        s_xeD = sem("s_xe_dve")
        s_gu = sem("s_gu")
        s_sg = sem("s_sg")
        s_hid = sem("s_hid")
        s_hhi = sem("s_hhi")
        s_hlo = sem("s_hlo")
        s_down = sem("s_down")
        s_y = sem("s_y")


        m_wr2, m_wsplit, m_used = {}, {}, {}

        def load_w(i):
            x_, which = divmod(i, 3)
            src = (w_gate, w_up, w_down)[which]
            if i >= RW:
                sp.wait(*m_wsplit[i - RW])
            m_wr2[i] = sp.do(lambda e: e.dma_start(wraw[:, i % RW], src[x_].rearrange("(k p) f -> p k f", p=P)),
                             s_wr[i % RW], 16)

        def split_w(i):
            r, t = i % RW, i % RS
            act.wait(m_wr2[i])
            if i >= RS:
                act.wait(m_used[i - RS])
            a = act.do(lambda e: e.activation(wsplit[:, t, 0], wraw[:, r], ACT.Copy), s_whi)
            eng, cnt = (pool, s_wloP) if i % 3 == 2 else (dve, s_wloD)
            eng.wait(a)
            d = eng.do(lambda e: e.tensor_tensor(wsplit[:, t, 1], wraw[:, r], wsplit[:, t, 0].bitcast(F32),
                                                 ALU.subtract), cnt)
            m_wsplit[i] = [a, d]

        m_xg, m_yb, m_xeturn, m_ys, m_xe = {}, {}, {}, {}, {}

        def gather(x_, n):
            p2 = x_ % 2
            dst, src, cnt, marks = ((xg, xn_rows, s_xg, m_xg), (yb, base_rows, s_yb, m_yb))[n]
            pool.wait(c_tab, c_clear_y if n else c_clear_x)
            if x_ >= 2:
                pool.wait((m_xeturn, m_ys)[n][x_ - 2])
            for r in range(NR):
                w = wide_of[r]
                marks[x_] = pool.do(lambda e, r=r, w=w: e.indirect_dma_start(
                    out=dst[0:w, p2, r, :], out_offset=None, in_=src[:, :],
                    in_offset=bass.IndirectOffsetOnAxis(ap=token_of[0:w, r, x_:x_ + 1], axis=0),
                    bounds_check=TOK - 1, oob_is_err=False), cnt[p2], 16)

        def turn_xe(x_, r):
            nonlocal misc_free
            p2 = x_ % 2
            pe.wait(m_xg[x_])
            w = wide_of[r]
            bank = p_misc
            pe.wait(*misc_free)
            for k in range(KT):
                m = pe.do(lambda e, r=r, w=w, k=k, bank=bank: e.transpose(
                    bank[:, k * w:(k + 1) * w], xg[0:w, p2, r, k * P:(k + 1) * P], ident[0:w, 0:w]),
                    s_xeP if k == KT - 1 else None)
            src = bank[:, 0:KT * w].rearrange("p (k t) -> p k t", k=KT)
            act.wait(m)
            if x_ >= 2:
                act.wait(m_gu_last[x_ - 2])
            hi = xe[:, p2, 0, :, r * P:r * P + w]
            lo = xe[:, p2, 1, :, r * P:r * P + w]
            a = act.do(lambda e, hi=hi, src=src: e.activation(hi, src, ACT.Copy), s_xeA)
            dve.wait(a)
            d = dve.do(lambda e, hi=hi, lo=lo, src=src: e.tensor_tensor(lo, src, hi.bitcast(F32), ALU.subtract),
                       s_xeD)
            misc_free = [a, d]
            m_xe.setdefault(x_, []).extend((a, d))
            m_xeturn[x_] = m

        m_gu_last, m_h = {}, {}
        gu_free = [[], []]
        h_free = []
        PARTS = ((0, 0), (0, 1), (1, 0))

        def gate_up(x_, f):
            n = x_ * KT + f
            r, p2 = n % 2, x_ % 2
            for which, bank in ((0, p_score), (1, p_turn)):
                i = 3 * x_ + which
                pe.wait(*m_wsplit[i], *m_xe[x_], *gu_free[r])
                terms = [(k, a, b) for k in range(KT) for a, b in PARTS]
                for j, (k, a, b) in enumerate(terms):
                    m = pe.do(lambda e, j=j, k=k, a=a, b=b, bank=bank, i=i: e.matmul(
                        bank[:, r, 0:CAP], wsplit[:, i % RS, a, k, f * P:(f + 1) * P], xe[:, p2, b, k, :],
                        start=j == 0, stop=j == len(terms) - 1), s_gu if j == len(terms) - 1 else None)
                m_used[i] = m
                if which == 0:
                    m_g = m
            m_gu_last[x_] = m
            g_, u_ = p_score[:, r, 0:CAP], p_turn[:, r, 0:CAP]
            act.wait(m_g)
            if n >= 2:
                act.wait(sg_marks[n - 2])
            a = act.do(lambda e: e.activation(sg[:, r], g_, ACT.Silu), s_sg)
            dve.wait(a, m)
            if n >= 2:
                dve.wait(m_h[n - 2][0])
            c = dve.do(lambda e: e.tensor_tensor(hid[:, r], sg[:, r], u_, ALU.mult), s_hid)
            sg_marks[n] = c
            gu_free[r] = [c]
            act.wait(c, *h_free)
            a = act.do(lambda e: e.activation(hparts[:, 0, f, :], hid[:, r], ACT.Copy), s_hhi)
            dve.wait(a)
            d = dve.do(lambda e: e.tensor_tensor(hparts[:, 1, f, :], hid[:, r], hparts[:, 0, f, :].bitcast(F32),
                                                 ALU.subtract), s_hlo)
            m_h[n] = [a, d]

        sg_marks = {}
        ybank = [p_proj[:, 0, :], p_proj[:, 1, :], p_att[:]]
        n_y = 0

        def down(x_):
            nonlocal n_y, h_free
            p2, i = x_ % 2, 3 * x_ + 2
            last = []
            for r in range(NR):
                w = wide_of[r]
                b2 = n_y % 3
                pe.wait(*m_wsplit[i], *y_free[b2])
                terms = [(f, a, b) for f in range(KT) for a, b in PARTS]
                for j, (f, a, b) in enumerate(terms):
                    pe.wait(*m_h[x_ * KT + f])
                    m = pe.do(lambda e, j=j, f=f, a=a, b=b, w=w, b2=b2, r=r: e.matmul(
                        ybank[b2][0:w, :], hparts[:, a, f, r * P:r * P + w], wsplit[:, i % RS, b, f, :],
                        start=j == 0, stop=j == len(terms) - 1), s_down if j == len(terms) - 1 else None)
                dve.wait(m, m_yb[x_])
                d = dve.do(lambda e, w=w, b2=b2, r=r: e.scalar_tensor_tensor(
                    out=yb[0:w, p2, r, :], in0=ybank[b2][0:w, :], scalar=gate_of[0:w, r, x_:x_ + 1],
                    in1=yb[0:w, p2, r, :], op0=ALU.mult, op1=ALU.add), s_y)
                y_free[b2] = [d]
                last.append(d)
                n_y += 1
            m_used[i] = m
            h_free = [m]
            pend.append((x_, last))

        pend = []

        def scatter(x_, last):
            p2 = x_ % 2
            for r in range(NR):
                w = wide_of[r]
                pool.wait(last[r])
                m_ys[x_] = pool.do(lambda e, r=r, w=w: e.indirect_dma_start(
                    out=out_rows[:, :], out_offset=bass.IndirectOffsetOnAxis(ap=token_of[0:w, r, x_:x_ + 1], axis=0),
                    in_=yb[0:w, p2, r, :], in_offset=None, bounds_check=TOK - 1, oob_is_err=False), s_ys[p2], 16)

        sp.wait(last_proj[NQ - 1])
        for i in range(RW):
            load_w(i)
        dve.wait(last_proj[NQ - 1])
        c_clear_x = dve.do(lambda e: e.memset(xg[:], 0.0), s_clear)
        pool.wait(*[m_xnst[tt] for tt in range((NQ - 1) * TPQ, NQ * TPQ)])
        gather(0, 0)
        gather(1, 0)
        step(NS - 1)
        end1 = [(c, c.value) for c in (
            s_const, s_scatter, s_ln, s_newton, s_resadd, s_xturn, s_xhi, s_xlo, s_proj, s_phi, s_plo, s_score,
            s_masked, s_negm, s_exp, s_turn, s_turnedA, s_turnedD, s_pm, s_ma, s_md, s_rt, s_load, s_bv, s_vst, s_pw,
            s_aw, s_dw, s_tab, *s_sum, *s_xnst, *s_x, *s_q, *s_k[0], *s_k[1], *s_v, s_copy, *s_wraw) if c.value]
        for eng in (act, dve):
            eng.wait(*end1)
        gu_free = [score_free[0] + turn_free[0], score_free[1] + turn_free[1]]
        split_w(0)
        load_w(RW)
        turn_xe(0, 0)
        step(NS)
        split_w(1)
        load_w(RW + 1)
        step(NS + 1)
        turn_xe(0, 1)
        split_w(2)
        load_w(RW + 2)
        turn_xe(0, 2)
        c_clear_y = dve.do(lambda e: e.memset(yb[:], 0.0), s_clear)
        s = NS + 2
        while late_jobs or late_stage:
            step(s)
            s += 1
        y_free = [proj_free[0], proj_free[1], att_free]
        pool.wait(*[m for t in range(NT) for m in ao_free[t]])
        gather(0, 1)

        def next_w(x_, which):
            i = 3 * (x_ + 1) + which
            if i < 3 * NX:
                split_w(i)
                if i + RW < 3 * NX:
                    load_w(i + RW)

        for x_ in range(NX):
            if x_ + 2 < NX:
                gather(x_ + 2, 0)
            next_w(x_, 0)
            for f in range(KT):
                gate_up(x_, f)
                if f == 1 and x_ + 1 < NX:
                    gather(x_ + 1, 1)
                if f and x_ + 1 < NX:
                    turn_xe(x_ + 1, f - 1)
            next_w(x_, 1)
            next_w(x_, 2)
            down(x_)
            scatter(*pend.pop())

        sp.wait(*[(c, c.value) for c in s_ys])

        block = ctx.enter_context(nc.Block())

        @block.tensor
        def _(e):
            pe.play(e)

        @block.scalar
        def _(e):
            act.play(e)

        @block.vector
        def _(e):
            dve.play(e)

        @block.gpsimd
        def _(e):
            pool.play(e)

        @block.sync
        def _(e):
            sp.play(e)


_INS = ["L0_attn_x", "L0_attn_Wq", "L0_attn_bq", "L0_attn_Wk", "L0_attn_bk", "L0_attn_Wv", "L0_attn_bv",
        "L0_ffn_w_router", "L0_ffn_w_gate", "L0_ffn_w_up", "L0_ffn_w_down"]


def kernel(**inputs):
    import concourse.bacc as bacc
    from concourse.bass_utils import run_bass_kernel_spmd

    nc = bacc.Bacc("TRN2", target_bir_lowering=False, num_devices=1)
    arrays, args = {}, []
    for name in _INS:
        a = np.ascontiguousarray(inputs[name])
        arrays[f"in_{name}"] = a
        args.append(nc.dram_tensor(f"in_{name}", a.shape, mybir.dt.from_np(a.dtype), kind="ExternalInput").ap())
    shape = inputs["L0_attn_x"].shape
    out = nc.dram_tensor("out_x", shape, F32, kind="ExternalOutput").ap()
    build(nc, *args, out)
    r = run_bass_kernel_spmd(nc, [arrays], core_ids=[0])
    return r.results[0]["out_x"]
```
